# Optimizing a Trainium2 kernel written in Bass

```python
import numpy as np
import jax
import jax.numpy as jnp

def _softmax(x, axis=-1):
    return jax.nn.softmax(x, axis=axis)

def _gelu(x):
    return jax.nn.gelu(x, approximate=True)

def _silu(x):
    return jax.nn.silu(x)

def _sigmoid(x):
    return jax.nn.sigmoid(x)

def _layernorm(x, axis=-1, eps=1e-05):
    m = jnp.mean(x, axis=axis, keepdims=True)
    v = jnp.var(x, axis=axis, keepdims=True)
    return (x - m) / jnp.sqrt(v + eps)

def _scatter_add(tgt, idx, src, axis=0):
    return tgt.at[idx].add(src)

def _segment_sum(src, seg, n):
    return jax.ops.segment_sum(src, seg, n)
kernel_name = 'mk_sandwich_d1_jaxref_r8_4956c6'

def setup_inputs(seed: int=0):
    np.random.seed(seed)
    _w = jnp.asarray

    def _L0_attn_setup():
        import jax, jax.numpy as jnp
        import numpy as np
        EMBED_DIM = 256
        NUM_HEADS = 32
        HEAD_DIM = EMBED_DIM // NUM_HEADS
        BATCH = 2
        SEQ_LEN = 256
        key = jax.random.key(seed)
        ks = jax.random.split(key, 5)
        scale = 1.0 / np.sqrt(EMBED_DIM)
        x = jax.random.normal(ks[0], (BATCH, SEQ_LEN, EMBED_DIM), dtype=jnp.float32)
        Wq = jax.random.normal(ks[1], (EMBED_DIM, EMBED_DIM), dtype=jnp.float32) * scale
        Wk = jax.random.normal(ks[2], (EMBED_DIM, EMBED_DIM), dtype=jnp.float32) * scale
        Wv = jax.random.normal(ks[3], (EMBED_DIM, EMBED_DIM), dtype=jnp.float32) * scale
        Wo = jax.random.normal(ks[4], (EMBED_DIM, EMBED_DIM), dtype=jnp.float32) * scale
        return {'x': x, 'Wq': Wq, 'Wk': Wk, 'Wv': Wv, 'Wo': Wo}
    _L0_attn_in = _L0_attn_setup()

    def _L0_ffn_setup():
        import jax, jax.numpy as jnp
        import numpy as np
        ALPHA = 1.702
        LIMIT = 7.0
        EPS = 1e-05
        TOP_K = 4
        key = jax.random.key(seed)
        ks = jax.random.split(key, 8)
        B, S, H, I, E = (2, 64, 256, 256, 16)
        return {'x': jax.random.normal(ks[0], (B, S, H), jnp.float32), 'norm_w': jnp.ones((H,), jnp.float32), 'gate_w': jax.random.normal(ks[1], (E, H), jnp.float32) * 0.02, 'gate_b': jax.random.normal(ks[2], (E,), jnp.float32) * 0.02, 'w1': jax.random.normal(ks[3], (E, 2 * I, H), jnp.float32) * 0.02, 'b1': jax.random.normal(ks[4], (E, 2 * I), jnp.float32) * 0.02, 'w2': jax.random.normal(ks[5], (E, H, I), jnp.float32) * 0.02, 'b2': jax.random.normal(ks[6], (E, H), jnp.float32) * 0.02}
    _L0_ffn_in = _L0_ffn_setup()
    _d = {'L0_attn_x': _L0_attn_in['x'], 'L0_attn_Wq': _L0_attn_in['Wq'], 'L0_attn_Wk': _L0_attn_in['Wk'], 'L0_attn_Wv': _L0_attn_in['Wv'], 'L0_attn_Wo': _L0_attn_in['Wo'], 'L0_ffn_norm_w': _L0_ffn_in['norm_w'], 'L0_ffn_gate_w': _L0_ffn_in['gate_w'], 'L0_ffn_gate_b': _L0_ffn_in['gate_b'], 'L0_ffn_w1': _L0_ffn_in['w1'], 'L0_ffn_b1': _L0_ffn_in['b1'], 'L0_ffn_w2': _L0_ffn_in['w2'], 'L0_ffn_b2': _L0_ffn_in['b2']}
    _x0 = _d['L0_attn_x']
    _d['L0_attn_x'] = jax.random.normal(jax.random.fold_in(jax.random.key(seed), 1), (4, 1024, 256), dtype=_x0.dtype)
    del _x0
    return _d

def reference(L0_attn_x, L0_attn_Wq, L0_attn_Wk, L0_attn_Wv, L0_attn_Wo, L0_ffn_norm_w, L0_ffn_gate_w, L0_ffn_gate_b, L0_ffn_w1, L0_ffn_b1, L0_ffn_w2, L0_ffn_b2):

    def _L0_attn_ref(x, Wq, Wk, Wv, Wo):
        import jax, jax.numpy as jnp
        import numpy as np
        EMBED_DIM = 256
        NUM_HEADS = 32
        HEAD_DIM = EMBED_DIM // NUM_HEADS
        BATCH = 2
        SEQ_LEN = 256
        q = jnp.einsum('bse,ef->bsf', x, Wq)
        k = jnp.einsum('bse,ef->bsf', x, Wk)
        v = jnp.einsum('bse,ef->bsf', x, Wv)
        qT = jnp.swapaxes(q, 1, 2)
        kT = jnp.swapaxes(k, 1, 2)
        vT = jnp.swapaxes(v, 1, 2)
        attn_scores = jnp.einsum('bes,bfs->bef', qT, kT) / np.sqrt(HEAD_DIM)
        attn_weights = jax.nn.softmax(attn_scores, axis=-1)
        attn_output = jnp.einsum('bef,bfs->bes', attn_weights, vT)
        attn_output = jnp.swapaxes(attn_output, 1, 2)
        return jnp.einsum('bse,ef->bsf', attn_output, Wo)

    def _L0_ffn_ref(x, norm_w, gate_w, gate_b, w1, b1, w2, b2):
        import jax, jax.numpy as jnp
        import numpy as np
        ALPHA = 1.702
        LIMIT = 7.0
        EPS = 1e-05
        TOP_K = 4
        B, S, H = x.shape
        M = B * S
        E = gate_w.shape[0]
        xf = x.reshape(M, H)
        t = xf * jax.lax.rsqrt(jnp.mean(xf * xf, axis=-1, keepdims=True) + EPS) * norm_w
        logits = t @ gate_w.T + gate_b
        vals, idx = jax.lax.top_k(logits, TOP_K)
        gates_k = jax.nn.softmax(vals, axis=-1)
        G = jnp.zeros((M, E), x.dtype).at[jnp.arange(M)[:, None], idx].set(gates_k)
        h = jnp.einsum('mh,eoh->emo', t, w1) + b1[:, None, :]
        a = jnp.minimum(h[..., ::2], LIMIT)
        b = jnp.clip(h[..., 1::2], -LIMIT, LIMIT)
        act = a * jax.nn.sigmoid(ALPHA * a) * (b + 1.0)
        y = jnp.einsum('emi,edi->emd', act, w2) + b2[:, None, :]
        delta = jnp.einsum('me,emd->md', G, y)
        return x + delta.reshape(B, S, H)
    x = L0_attn_x
    x = x + _layernorm(_L0_attn_ref(_layernorm(x, axis=-1), L0_attn_Wq, L0_attn_Wk, L0_attn_Wv, L0_attn_Wo), axis=-1)
    x = x + _layernorm(_L0_ffn_ref(_layernorm(x, axis=-1), L0_ffn_norm_w, L0_ffn_gate_w, L0_ffn_gate_b, L0_ffn_w1, L0_ffn_b1, L0_ffn_w2, L0_ffn_b2), axis=-1)
    return x

_drawn_inputs = setup_inputs


def setup_inputs(seed=0):
    import zlib

    import numpy as np

    out = dict(_drawn_inputs(seed))
    spreads = {'L0_ffn_norm_w': (1.0, 0.6)}
    factors = {'L0_ffn_gate_w': 4.814,
     'L0_ffn_gate_b': 8.0,
     'L0_ffn_w1': 4.48,
     'L0_ffn_b1': 8.0,
     'L0_ffn_w2': 4.328,
     'L0_ffn_b2': 27.069}
    for name, (base, spread) in spreads.items():
        noise = np.random.default_rng([zlib.crc32(name.encode()), seed]).standard_normal(out[name].shape)
        drawn = base * np.exp(spread * noise) if base else spread * noise
        out[name] = jnp.asarray(drawn.astype(out[name].dtype))
    for name, factor in factors.items():
        out[name] = (out[name] * factor).astype(out[name].dtype)
    return out
```

```python
from contextlib import ExitStack

import concourse.bass as bass
from concourse import mybir

ALU = mybir.AluOpType
ACT = mybir.ActivationFunctionType
AX_X = mybir.AxisListType.X
F32 = mybir.dt.float32
F16 = mybir.dt.float16
BF16 = mybir.dt.bfloat16
I32 = mybir.dt.int32
U32 = mybir.dt.uint32

P = 128
EPS = 1e-5
LIMIT = 7.0
ALPHA = 1.702
TOP = 4
HEADS = 32
U_SCALE = 64.0
W_SCALE = 256.0
A_SCALE = 64.0
H_SCALE = U_SCALE * W_SCALE
Y_SCALE = A_SCALE * W_SCALE


def wait(engine, semaphore, value):
    if not isinstance(value, int) or value > 0:
        engine.wait_ge(semaphore, value)


class Steps:

    def __init__(self, engine, semaphore):
        self.engine, self.semaphore, self.base, self.n = engine, semaphore, 0, 0

    def link(self, instruction, apart=None):
        self.n += 1
        instruction.then_inc(self.semaphore, 1)
        self.engine.wait_ge(self.semaphore, self.base + self.n)
        if apart:
            apart(self.engine)

    def passed(self):
        self.base, self.n = self.base + self.n, 0
        return self.base


def moe_block(nc, x, wq, wk, wv, wo, norm_w, gate_w, gate_b, w1, b1, w2, b2, out):
    B, S, D = x.shape
    E, O, _ = w1.shape
    C = D // P
    assert C == 2 and O == 2 * D and w2.shape == (E, D, D) and S % P == 0
    TB = S // P
    N = B * S
    REGION = N + P
    RING = 8
    STEPS = -(-(N * TOP // P + E - 1) // RING) * RING
    ROUNDS = STEPS // RING
    ROW = D + 2
    PLACE, GATE = D, D + 1
    PAIRS = N * TOP
    W1PART = C * O
    W2PART = C * D
    PICK = 2 * (W1PART + W2PART)
    WE = PICK + P
    SCORE_SCALE = float(D // HEADS) ** -0.5
    ROW_MAX = E * REGION

    x_dram = x.rearrange("b (p j) d -> (b p) (j d)", p=P)
    out_dram = out.rearrange("b (p j) d -> (b p) (j d)", p=P)
    rows = nc.dram_tensor("expert_rows", [(E + 1) * REGION, ROW], F32).ap()
    results = nc.dram_tensor("expert_results", [PAIRS, D], F32).ap()
    results_dram = results.rearrange("(q t) d -> q (t d)", t=TB * TOP)

    with ExitStack() as ctx:
        def sb(name, shape, dt=F32):
            return ctx.enter_context(nc.sbuf_tensor(name, shape, dt))

        def sem(name):
            return ctx.enter_context(nc.semaphore(name))

        X = sb("X", [P, B * TB * D])
        W = sb("W", [P, E * WE], F16)
        bias_rows = sb("bias_rows", [96, O + D], BF16)
        ident = sb("ident", [P, P])
        ident16 = sb("ident16", [P, P], F16)
        below = sb("below", [P, P], BF16)
        ones = sb("ones", [P, P], BF16)
        wqs = sb("wqs", [P, C, D])
        wks = sb("wks", [P, C, D])
        wvT = sb("wvT", [P, C, D])
        wos = sb("wos", [P, C, D])
        gateT = sb("gateT", [P, C, E])
        gate_b_all = sb("gate_b_all", [P, E])
        norm = sb("norm", [P, C])
        norm_scaled = sb("norm_scaled", [P, C])
        pow_half = sb("pow_half", [P, TB])
        expert_no = sb("expert_no", [P, E])
        place = sb("place", [P, B * TB * TOP], I32)
        zero_rows = sb("zero_rows", [P, ROW])
        step_at = sb("step_at", [1, STEPS], I32)
        step_row = sb("step_row", [1, STEPS], I32)
        pad_row = sb("pad_row", [1, E + 1], I32)
        ffn_rstd = sb("ffn_rstd", [P, B * TB])
        ffn_bias = sb("ffn_bias", [P, B * TB])
        stats = sb("stats", [P, TB, 6])
        mv = sb("mv", [P, TB, 2])
        var_eps = sb("var_eps", [P, TB])
        rstd = sb("rstd", [P, TB])
        mean_sq = sb("mean_sq", [P, TB])
        rms = sb("rms", [P, TB])
        u_mult = sb("u_mult", [P, TB])
        row_max = sb("row_max", [P, C])
        row_neg = sb("row_neg", [P, C])
        row_sum = sb("row_sum", [P, C])
        row_inv = sb("row_inv", [P, C])
        wo_mean = sb("wo_mean", [P, C])
        logits = sb("logits", [P, TB, E])
        top_v = sb("top_v", [P, TB, 8])
        top_i = sb("top_i", [P, TB, 8], U32)
        top_f = sb("top_f", [P, TB, TOP])
        gate_e = sb("gate_e", [P, TB, TOP])
        gate_sum = sb("gate_sum", [P, TB])
        gate_inv = sb("gate_inv", [P, TB])
        gates = sb("gates", [P, TB, TOP])
        onehot = sb("onehot", [P, TB * TOP, E])
        chosen = sb("chosen", [P, TB, E], BF16)
        batch_count = sb("batch_count", [P, E])
        count = sb("count", [P, E], BF16)
        rank = sb("rank", [P, TB * TOP])
        row_f = sb("row_f", [P, TB * TOP])
        row_i = sb("row_i", [P, TB * TOP], U32)
        stage = sb("stage", [P, 2, TOP, ROW])
        raw1 = sb("raw1", [P, 2, C, O])
        raw2 = sb("raw2", [P, 2, C, D])
        cum = sb("cum", [P, 2, E])
        tile_f = sb("tile_f", [P, E])
        tile_i = sb("tile_i", [P, E], I32)
        step_f = sb("step_f", [1, 4, STEPS])
        pad_f = sb("pad_f", [1, E + 1])
        pad_base = sb("pad_base", [1, E + 1])
        AREA = 4 * S // P * D
        area = sb("area", [P, AREA])

        def views(sizes, of=area, dt=F32):
            at, made = 0, []
            for n in sizes:
                made.append(of[:, at:at + n])
                at += n
            assert at <= of.shape[1]
            return made

        XN, xnT, gram, prod, probs, mixer, uT = views([TB * D, C * S, C * D, C * D, C * D, C * D, 2 * 512])
        XN = XN.rearrange("p (j d) -> p j d", j=TB)
        xnT, gram, prod, probs, mixer = (
            v.rearrange("p (c d) -> p c d", c=C) for v in (xnT, gram, prod, probs, mixer))
        uT = uT.rearrange("p (r n) -> p r n", r=2)
        table = area[0:1, 0:STEPS * E].rearrange("p (s e) -> p s e", e=E)
        tiles, utp, a_t, b_t, sig_t, m_t, act_t, act_hl, actT, y_t = views(
            [RING * ROW, 2 * D, 2 * D, 2 * D, 2 * D, 2 * D, 2 * D, 2 * D, 2 * D, 4 * D])
        tiles = tiles.rearrange("p (r n) -> p r n", r=RING)
        utp, act_hl, actT = (
            v.bitcast(F16).rearrange("p (r n) -> p r n", r=2) for v in (utp, act_hl, actT))
        a_t, b_t, sig_t, m_t, act_t = (
            v.rearrange("p (r n) -> p r n", r=2) for v in (a_t, b_t, sig_t, m_t, act_t))
        y_t = y_t.rearrange("p (r n) -> p r n", r=4)
        got, part, ffn, summed_t, fin = views(
            [TB * TOP * D, TB * 2 * D, TB * D, TB * D, TB * D], of=W[:, :].bitcast(F32))
        got = got.rearrange("p (j n) -> p j n", j=TB)
        part = part.rearrange("p (j n) -> p j n", j=TB)
        ffn, summed_t, fin = (v.rearrange("p (j d) -> p j d", j=TB) for v in (ffn, summed_t, fin))
        picks = W[0:96, :].bitcast(BF16).rearrange("p (e w) -> p e w", e=E)[:, :, PICK:PICK + P]
        wv_raw = raw2[:, 0]
        gate_raw = raw1[0:E, 0, 0, 0:D]
        wo_raw = raw2[:, 1]
        bias_f = raw1[0:96, 1].rearrange("p c n -> p (c n)")[:, 0:O + D]
        bias_t = raw1[0:96, 0].rearrange("p c n -> p (c n)")[:, 0:O + D]

        bank = [ctx.enter_context(nc.psum_tensor(f"bank{i}", [P, 512], F32)) for i in range(8)]

        x_loaded = sem("x_loaded")
        attn_w_loaded = sem("attn_w_loaded")
        setup_loaded = sem("setup_loaded")
        bias_loaded = sem("bias_loaded")
        raw_loaded = [sem(f"raw_loaded{i}") for i in range(2)]
        rows_sent = [sem(f"rows_sent{i}") for i in range(2)]
        pads_written = sem("pads_written")
        tile_loaded = [sem(f"tile_loaded{i}") for i in range(RING)]
        result_sent = [sem(f"result_sent{i}") for i in range(RING)]
        got_loaded = [sem(f"got_loaded{i}") for i in range(TB)]
        out_stored = sem("out_stored")
        wait_over = sem("wait_over")
        consts = sem("consts")
        pool_first = sem("pool_first")
        bias_zeroed = sem("bias_zeroed")
        setup_turned = sem("setup_turned")
        wv_turned_copied = sem("wv_turned_copied")
        setup_done = sem("setup_done")
        bias_ready = sem("bias_ready")
        dve_step = sem("dve_step")
        var_ready = sem("var_ready")
        rstd_ready = sem("rstd_ready")
        xn_ready = sem("xn_ready")
        gram_done = sem("gram_done")
        gram_copied = sem("gram_copied")
        xn_turned = sem("xn_turned")
        xnT_copied = sem("xnT_copied")
        prod_done = sem("prod_done")
        prod_copied = sem("prod_copied")
        scores_done = sem("scores_done")
        max_ready = sem("max_ready")
        exp_done = sem("exp_done")
        probs_ready = sem("probs_ready")
        mixer_done = sem("mixer_done")
        mixer_copied = sem("mixer_copied")
        att_done = sem("att_done")
        u_ready = sem("u_ready")
        hi_staged = sem("hi_staged")
        u_turned_front = sem("u_turned_front")
        uT_copied_front = sem("uT_copied_front")
        logits_done = sem("logits_done")
        gate_in_ready = sem("gate_in_ready")
        gate_exp_done = sem("gate_exp_done")
        chosen_ready = sem("chosen_ready")
        rank_done = sem("rank_done")
        staged = sem("staged")
        w_turned = sem("w_turned")
        w_high = sem("w_high")
        w_low = sem("w_low")
        counts_done = sem("counts_done")
        counted = sem("counted")
        tables_ready = sem("tables_ready")
        pad_ready = sem("pad_ready")
        u_turned = sem("u_turned")
        u_copied = sem("u_copied")
        h_done = sem("h_done")
        a_ready = sem("a_ready")
        h_used = sem("h_used")
        m_ready = sem("m_ready")
        sig_ready = sem("sig_ready")
        act_ready = sem("act_ready")
        high_ready = sem("high_ready")
        low_ready = sem("low_ready")
        act_turned = sem("act_turned")
        act_copied = sem("act_copied")
        y_done = sem("y_done")
        y_ready = sem("y_ready")
        ffn_in_ready = sem("ffn_in_ready")
        pairs_added = sem("pairs_added")
        ffn_summed = sem("ffn_summed")
        shifted = sem("shifted")
        scaled = sem("scaled")
        got_used = sem("got_used")

        block = ctx.enter_context(nc.Block())

        def tile_x(b, j):
            return X[:, bass.ds(b * (TB * D) + j * D, D)]

        def halves(i):
            return [bank[i][:, 0:D], bank[i][:, D:2 * D]]

        def apart(engine):
            engine.sem_inc(wait_over, 1)

        def live(s):
            return not isinstance(s, int) or 0 <= s < STEPS

        @block.sync
        def _(sp):
            for b in range(B):
                wait(sp, x_loaded, 16 * b)
                sp.dma_start(X[:, b * TB * D:(b + 1) * TB * D], x_dram[b * P:(b + 1) * P, :]).then_inc(x_loaded, 16)
                if b == 0:
                    for w, to in ((wk, wks), (wq, wqs)):
                        sp.dma_start(to[:], w.rearrange("(c p) f -> p c f", p=P)).then_inc(attn_w_loaded, 16)
                    for w, to in ((wv, wv_raw), (wo, wo_raw)):
                        sp.dma_start(to, w.rearrange("(c p) f -> p c f", p=P)).then_inc(setup_loaded, 16)
                    sp.dma_start(gate_raw, gate_w).then_inc(setup_loaded, 16)
                    sp.dma_start(norm[:], norm_w.rearrange("(c p) -> p c", p=P),
                                 allow_slow_non_contiguous=True).then_inc(setup_loaded, 16)
                    sp.dma_start(gate_b_all[:], gate_b.partition_broadcast(P)).then_inc(setup_loaded, 16)
                    sp.wait_ge(bias_zeroed, 1)
                    for part_no in range(3):
                        to = bias_f[32 * part_no:32 * part_no + E, :]
                        sp.dma_start(to[:, 0:O], b1).then_inc(bias_loaded, 16)
                        sp.dma_start(to[:, O:O + D], b2).then_inc(bias_loaded, 16)

            sp.wait_ge(setup_done, 1)
            sp.wait_ge(bias_ready, 3)

            def load_expert(e, r):
                wait(sp, w_low, 3 * (e - 1))
                for q in range(C):
                    w1_e = w1.rearrange("e (r c) h -> (e r) (c h)", c=2)
                    sp.dma_start(raw1[:, r, q, :], w1_e[bass.ds(e * D + q * P, P), :]).then_inc(raw_loaded[r], 16)
                    w2_e = w2.rearrange("e d i -> (e d) i")
                    sp.dma_start(raw2[:, r, q, :], w2_e[bass.ds(e * D + q * P, P), :]).then_inc(raw_loaded[r], 16)

            for r in range(2):
                load_expert(r, r)
            with sp.Fori(1, E // 2) as k:
                for r in range(2):
                    load_expert(k * 2 + r, r)

            sp.wait_ge(pad_ready, 1)
            with sp.Fori(0, E + 1) as e:
                at = sp.value_load(pad_row[0:1, bass.ds(e, 1)], min_val=0, max_val=ROW_MAX)
                sp.dma_start(rows[bass.ds(at, P), :], zero_rows[:]).then_inc(pads_written, 16)
            sp.wait_ge(tables_ready, 1)
            sp.wait_ge(pads_written, 16 * (E + 1))
            for i in range(2):
                sp.wait_ge(rows_sent[i], 16 * TOP * B * TB // 2)

            def load_tile(m, c):
                at = sp.value_load(step_row[0:1, bass.ds(m * RING + c, 1)], min_val=0, max_val=ROW_MAX)
                wait(sp, result_sent[c], 16 * m)
                sp.dma_start(tiles[:, c, :], rows[bass.ds(at, P), :]).then_inc(tile_loaded[c], 16)

            for c in range(RING):
                load_tile(0, c)
            with sp.Fori(1, ROUNDS) as m:
                for c in range(RING):
                    load_tile(m, c)

            for c in range(RING):
                sp.wait_ge(result_sent[c], 16 * ROUNDS)

            def load_results(b, j):
                wait(sp, pairs_added, (b - 1) * TB + j + 1)
                sp.dma_start(got[:, j, :], results_dram[bass.ds(b * P, P), j * TOP * D:(j + 1) * TOP * D]
                             ).then_inc(got_loaded[j], 16)

            def store(b):
                sp.wait_ge(scaled, (b + 1) * TB)
                sp.dma_start(out_dram[bass.ds(b * P, P), :], fin.rearrange("p j d -> p (j d)")).then_inc(out_stored, 16)

            for j in range(TB):
                load_results(0, j)
            with sp.Fori(1, B) as b:
                for j in range(TB):
                    load_results(b, j)
                store(b - 1)
            store(B - 1)
            sp.wait_ge(out_stored, 16 * B)

        @block.gpsimd
        def _(pool):
            pool.memset(raw1[:, 1], 0.0).then_inc(bias_zeroed, 1)
            pool.memset(pow_half[:], -0.5).then_inc(consts, 1)
            pool.memset(ident[:], 0.0).then_inc(pool_first, 1)
            pool.wait_ge(pool_first, 1)
            pool.affine_select(out=ident[:], in_=ident[:], compare_op=ALU.not_equal, fill=1.0, base=0,
                               pattern=[[-1, P]], channel_multiplier=1).then_inc(consts, 1)
            pool.memset(ones[:], 1.0).then_inc(pool_first, 1)
            pool.wait_ge(pool_first, 2)
            pool.affine_select(out=below[:], in_=ones[:], compare_op=ALU.is_gt, fill=0.0, base=0,
                               pattern=[[1, P]], channel_multiplier=-1).then_inc(consts, 1)
            pool.iota(expert_no[:], pattern=[[1, E]], base=0, channel_multiplier=0,
                      allow_small_or_imprecise_dtypes=True).then_inc(consts, 1)
            pool.iota(place[:].rearrange("p (b t) -> p b t", b=B), pattern=[[P * TB * TOP, B], [1, TB * TOP]],
                      base=0, channel_multiplier=TB * TOP).then_inc(consts, 1)
            pool.memset(picks, 0.0).then_inc(pool_first, 1)
            for part_no in range(3):
                pool.wait_ge(pool_first, 3 + part_no)
                pool.affine_select(out=picks, in_=picks, compare_op=ALU.not_equal, fill=1.0, base=-32 * part_no,
                                   pattern=[[-1, E], [0, P]], channel_multiplier=1).then_inc(pool_first, 1)
            pool.memset(zero_rows[:, 0:D], 0.0).then_inc(consts, 1)
            pool.memset(zero_rows[:, GATE:GATE + 1], 0.0).then_inc(consts, 1)
            pool.iota(zero_rows[:, PLACE:PLACE + 1].bitcast(I32), pattern=[[0, 1]], base=PAIRS,
                      channel_multiplier=0).then_inc(consts, 1)
            pool.iota(step_f[:, 0, :], pattern=[[1, STEPS]], base=0, channel_multiplier=0,
                      allow_small_or_imprecise_dtypes=True).then_inc(consts, 1)
            pool.iota(pad_base[:], pattern=[[REGION, E + 1]], base=0, channel_multiplier=0,
                      allow_small_or_imprecise_dtypes=True).then_inc(consts, 1)

            def power(n):
                pool.wait_ge(var_ready, n)
                pool.tensor_tensor(rstd[:], var_eps[:], pow_half[:], ALU.pow).then_inc(rstd_ready, 1)

            def batch(b):
                for n in range(4):
                    power(4 * b + n + 1)
                for j in range(TB):
                    pool.wait_ge(staged, TB * b + j + 1)
                    apart(pool)
                    for k in range(TOP):
                        pool.indirect_dma_start(
                            rows, bass.IndirectOffsetOnAxis(ap=row_i[:, j * TOP + k:j * TOP + k + 1], axis=0),
                            stage[:, j % 2, k, :], None).then_inc(rows_sent[j % 2], 16)

            batch(0)
            with pool.Fori(1, B) as b:
                batch(b)

            def send(m, c):
                pool.wait_ge(y_ready, m * RING + c + 1)
                apart(pool)
                pool.indirect_dma_start(
                    results, bass.IndirectOffsetOnAxis(ap=tiles[:, c, PLACE:PLACE + 1].bitcast(U32), axis=0),
                    y_t[:, c % 4, :], None, bounds_check=last_place, oob_is_err=False).then_inc(result_sent[c], 16)

            last_place = pool.to_reg(PAIRS - 1)
            with pool.Fori(0, ROUNDS) as m:
                for c in range(RING):
                    send(m, c)

            def end(b):
                for j in range(TB):
                    pool.wait_ge(got_loaded[j], 16 * (b + 1))
                    wait(pool, ffn_summed, 2 * ((b - 1) * TB + j + 1))
                    pool.tensor_tensor(part[:, j, :], got[:, j, 0:2 * D], got[:, j, 2 * D:4 * D],
                                       ALU.add).then_inc(pairs_added, 1)
                power(4 * B + b + 1)

            end(0)
            with pool.Fori(1, B) as b:
                end(b)

        @block.scalar
        def _(act):
            def copy(to, of):
                return act.activation(to, of, ACT.Copy)

            act.wait_ge(setup_turned, 1)
            copy(wvT[:].rearrange("p c d -> p (c d)"), bank[6][:, :]).then_inc(wv_turned_copied, 1)

            def batch(b):
                act.wait_ge(gram_done, b + 1)
                copy(gram.rearrange("p c d -> p (c d)"), bank[4][:, :]).then_inc(gram_copied, 1)
                for t in range(TB // 2):
                    act.wait_ge(xn_turned, TB // 2 * b + t + 1)
                    copy(xnT[:, :, t * 2 * P:(t + 1) * 2 * P],
                         bank[6 + t % 2][:, :].rearrange("p (c n) -> p c n", c=C)).then_inc(xnT_copied, 1)
                act.wait_ge(prod_done, 2 * b + 1)
                copy(prod.rearrange("p c d -> p (c d)"), bank[5][:, :]).then_inc(prod_copied, 1)
                act.wait_ge(max_ready, b + 1)
                for c in range(C):
                    last = act.activation(probs[:, c, :], halves(4)[c], ACT.Exp, bias=row_neg[:, c:c + 1],
                                          scale=SCORE_SCALE, accum_out=row_sum[:, c:c + 1])
                last.then_inc(exp_done, 1)
                act.wait_ge(prod_done, 2 * b + 2)
                copy(prod.rearrange("p c d -> p (c d)"), bank[5][:, :]).then_inc(prod_copied, 1)
                act.wait_ge(mixer_done, b + 1)
                copy(mixer.rearrange("p c d -> p (c d)"), bank[4][:, :]).then_inc(mixer_copied, 1)
                for t in range(TB // 2):
                    act.wait_ge(u_turned_front, TB // 2 * b + t + 1)
                    wait(act, logits_done, TB // 2 * b + t - 1)
                    copy(uT[:, t % 2, :], bank[6 + t % 2][:, :]).then_inc(uT_copied_front, 1)
                act.wait_ge(gate_in_ready, b + 1)
                act.activation(gate_e[:], gate_e[:], ACT.Exp).then_inc(gate_exp_done, 1)
                for j in range(TB):
                    act.wait_ge(u_ready, TB * b + j + 1)
                    wait(act, rows_sent[j % 2], 16 * TOP * (TB // 2 * b + j // 2))
                    copy(stage[:, j % 2, 0, 0:P].bitcast(F16), XN[:, j, :]).then_inc(hi_staged, 1)

            batch(0)
            with act.Fori(1, B) as b:
                batch(b)

            def expert(e, r, at):
                for c in range(C):
                    act.wait_ge(w_turned, 3 * e + c + 1)
                    act.activation(W[:, bass.ds(at + c * O, O)], bank[3 * r + c][:, :], ACT.Copy,
                                   scale=norm_scaled[:, c:c + 1]).then_inc(w_high, 1)
                act.wait_ge(w_turned, 3 * e + 3)
                act.activation(W[:, bass.ds(at + 2 * W1PART, W2PART)], bank[3 * r + 2][:, :], ACT.Copy,
                               scale=W_SCALE).then_inc(w_high, 1)

            with act.Fori(0, E // 2) as k:
                for r in range(2):
                    expert(k * 2 + r, r, k * (2 * WE) + r * WE)

            def step(m, c):
                s = m * RING + c
                if live(s):
                    act.wait_ge(u_turned, s + 1)
                    wait(act, h_done, s - 1)
                    act.copy(utp[:, c % 2, :], bank[c % 2][:, :].bitcast(F16)[:, 0:4 * P]).then_inc(u_copied, 1)
                if live(s - 2):
                    act.wait_ge(act_ready, s - 1)
                    wait(act, act_turned, s - 3)
                    copy(act_hl[:, c % 2, 0:D], act_t[:, c % 2, :]).then_inc(high_ready, 1)
                if live(s - 1):
                    act.wait_ge(a_ready, s)
                    act.activation(sig_t[:, (c - 1) % 2, :], a_t[:, (c - 1) % 2, :], ACT.Sigmoid,
                                   scale=ALPHA).then_inc(sig_ready, 1)
                if live(s - 5):
                    act.wait_ge(y_done, s - 4)
                    q, slot = divmod(c - 9, RING)
                    wait(act, result_sent[slot], 16 * (m + q + 1))
                    act.activation(y_t[:, (c - 5) % 4, :], bank[6 + (c - 5) % 2][:, 0:D], ACT.Copy,
                                   scale=tiles[:, (c - 5) % RING, GATE:GATE + 1]).then_inc(y_ready, 1)

            for c in range(RING):
                step(0, c)
            with act.Fori(1, ROUNDS) as m:
                for c in range(RING):
                    step(m, c)
            for c in range(5):
                step(ROUNDS, c)

            for c in range(RING):
                act.wait_ge(result_sent[c], 16 * ROUNDS)

            def end(b):
                for j in range(TB):
                    wait(act, ffn_summed, 2 * ((b - 1) * TB + j + 1))
                    act.activation(ffn[:, j, :], tile_x(b, j), ACT.Identity,
                                   scale=ffn_rstd[:, bass.ds(b * TB + j, 1)],
                                   bias=ffn_bias[:, bass.ds(b * TB + j, 1)]).then_inc(ffn_in_ready, 1)

            end(0)
            with act.Fori(1, B) as b:
                end(b)

        @block.tensor
        def _(pe):
            pe.wait_ge(consts, 2)
            pe.wait_ge(setup_loaded, 16 * 5)
            for f in range(C):
                for h in range(C):
                    last = pe.transpose(bank[6][:, f * D + h * P:f * D + (h + 1) * P],
                                        wv_raw[:, h, f * P:(f + 1) * P], ident[:, :])
            last.then_inc(setup_turned, 1)
            for h in range(C):
                last = pe.transpose(bank[7][:, h * E:(h + 1) * E], gate_raw[:, h * P:(h + 1) * P],
                                    ident[0:E, 0:E])
            last.then_inc(setup_turned, 1)
            pe.wait_ge(wv_turned_copied, 1)
            pe.wait_ge(setup_done, 1)
            pe.wait_ge(attn_w_loaded, 32)

            def batch(b):
                pe.wait_ge(xn_ready, TB * (b + 1))
                for h in range(C):
                    for j in range(TB):
                        last = pe.matmul(halves(4)[h], XN[:, j, h * P:(h + 1) * P], XN[:, j, :],
                                         start=(j == 0), stop=(j == TB - 1))
                last.then_inc(gram_done, 1)
                for t in range(TB // 2):
                    wait(pe, xnT_copied, TB // 2 * b + t - 1)
                    for c in range(C):
                        for j in range(2):
                            last = pe.transpose(bank[6 + t % 2][:, (2 * c + j) * P:(2 * c + j + 1) * P],
                                                XN[:, 2 * t + j, c * P:(c + 1) * P], ident[:, :])
                    last.then_inc(xn_turned, 1)

                def square(to, left, right):
                    for m in range(C):
                        for c in range(C):
                            last = pe.matmul(halves(to)[m], left[:, c, m * P:(m + 1) * P], right[:, c, :],
                                             start=(c == 0), stop=(c == C - 1))
                    return last

                pe.wait_ge(gram_copied, b + 1)
                square(5, gram, wks).then_inc(prod_done, 1)
                pe.wait_ge(prod_copied, 2 * b + 1)
                square(4, wqs, prod).then_inc(scores_done, 1)
                pe.wait_ge(probs_ready, b + 1)
                square(5, probs, wos).then_inc(prod_done, 1)
                pe.wait_ge(prod_copied, 2 * b + 2)
                square(4, wvT, prod).then_inc(mixer_done, 1)
                pe.wait_ge(mixer_copied, b + 1)
                for j in range(TB):
                    for c in range(C):
                        last = pe.matmul(halves(j // 2)[j % 2], xnT[:, c, j * P:(j + 1) * P], mixer[:, c, :],
                                         start=(c == 0), stop=(c == C - 1))
                    if j % 2:
                        last.then_inc(att_done, 1)

                def turn(t):
                    pe.wait_ge(u_ready, TB * b + 2 * t + 2)
                    wait(pe, uT_copied_front, TB // 2 * b + t - 1)
                    for j in range(2):
                        for c in range(C):
                            last = pe.transpose(bank[6 + t % 2][:, (2 * j + c) * P:(2 * j + c + 1) * P],
                                                XN[:, 2 * t + j, c * P:(c + 1) * P], ident[:, :])
                    last.then_inc(u_turned_front, 1)

                def route(t):
                    pe.wait_ge(uT_copied_front, TB // 2 * b + t + 1)
                    for j in range(2):
                        for c in range(C):
                            last = pe.matmul(bank[5][:, (2 * t + j) * E:(2 * t + j + 1) * E],
                                             uT[:, t % 2, (2 * j + c) * P:(2 * j + c + 1) * P], gateT[:, c, :],
                                             start=(c == 0), stop=(c == C - 1))
                    last.then_inc(logits_done, 1)

                turn(0)
                for t in range(1, TB // 2):
                    turn(t)
                    route(t - 1)
                route(TB // 2 - 1)

                pe.wait_ge(chosen_ready, b + 1)
                ranks = bank[4][:, 0:TB * E].rearrange("p (j e) -> p j e", e=E)
                pe.matmul(ranks, below[:, :], chosen[:, :, :], start=True, stop=False)
                for j in range(TB - 1):
                    pe.matmul(ranks[:, j + 1:TB, :], ones[:, :],
                              chosen[:, j:j + 1, :].to_broadcast([P, TB - 1 - j, E]), start=False, stop=False,
                              skip_group_check=True)
                pe.matmul(ranks, ones[:, :], count[:, :].unsqueeze(1).to_broadcast([P, TB, E]),
                          start=False, stop=True).then_inc(rank_done, 1)

            batch(0)
            with pe.Fori(1, B) as b:
                batch(b)

            pe.wait_ge(counted, B)
            pe.matmul(bank[7][:, 0:E], ones[:, :], count[:, :], start=True, stop=True).then_inc(counts_done, 1)

            def expert(e, r, loaded):
                pe.wait_ge(raw_loaded[r], loaded)
                for c in range(C):
                    wait(pe, w_low, 3 * (e - 2) + c + 1)
                    for ab in range(2):
                        for q in range(C):
                            last = pe.transpose(bank[3 * r + c][:, ab * D + q * P:ab * D + (q + 1) * P],
                                                raw1[:, r, q, ab * D + c * P:ab * D + (c + 1) * P], ident[:, :])
                    last.then_inc(w_turned, 1)
                wait(pe, w_low, 3 * (e - 2) + 3)
                for c in range(C):
                    for q in range(C):
                        last = pe.transpose(bank[3 * r + 2][:, c * D + q * P:c * D + (q + 1) * P],
                                            raw2[:, r, q, c * P:(c + 1) * P], ident[:, :])
                last.then_inc(w_turned, 1)

            for r in range(2):
                expert(r, r, 16 * 4)
            with pe.Fori(1, E // 2) as k:
                for r in range(2):
                    expert(k * 2 + r, r, k * 64 + 64)

            pe.wait_ge(tables_ready, 1)
            pe.wait_ge(w_low, 3 * E)
            pe.wait_ge(bias_ready, 3)

            def turn_rows(s, c):
                pe.wait_ge(tile_loaded[c % RING], 16 * (s // RING + 1) if isinstance(s, int) else (s - c) * 2 + 16)
                wait(pe, u_copied, s - 1)
                of = tiles[:, c % RING, 0:D].bitcast(F16)
                to = bank[c % 2][:, :].bitcast(F16)
                for k in range(4):
                    last = pe.transpose(to[:, k * P:(k + 1) * P], of[:, k * P:(k + 1) * P], ident16[:, :])
                last.then_inc(u_turned, 1)

            def first(s, c, at):
                pe.wait_ge(u_copied, s + 1)
                wait(pe, h_used, s - 1)
                to = bank[2 + c % 2][:, :]
                pe.matmul(to, W[0:96, bass.ds(at + PICK, P)].bitcast(BF16), bias_rows[:, 0:O], start=True, stop=False)
                n = 0
                for h in range(C):
                    for u_part, w_part in ((0, 0), (1, 0), (0, 1)):
                        n += 1
                        last = pe.matmul(to, utp[:, c % 2, (2 * u_part + h) * P:(2 * u_part + h + 1) * P],
                                         W[:, bass.ds(at + (w_part * W1PART + h * O), O)],
                                         start=False, stop=(n == 3 * C))
                last.then_inc(h_done, 1)

            def turn_act(s, c):
                pe.wait_ge(low_ready, s + 1)
                wait(pe, act_copied, s - 1)
                to = bank[4 + c % 2][:, :].bitcast(F16)
                for k in range(4):
                    last = pe.transpose(to[:, k * P:(k + 1) * P], act_hl[:, c % 2, k * P:(k + 1) * P], ident16[:, :])
                last.then_inc(act_turned, 1)

            def second(s, c, at):
                pe.wait_ge(act_copied, s + 1)
                wait(pe, y_ready, s - 1)
                to = bank[6 + c % 2][:, 0:D]
                pe.matmul(to, W[0:96, bass.ds(at + PICK, P)].bitcast(BF16), bias_rows[:, O:O + D],
                          start=True, stop=False)
                n = 0
                for h in range(C):
                    for a_part, w_part in ((0, 0), (1, 0), (0, 1)):
                        n += 1
                        last = pe.matmul(to, actT[:, c % 2, (2 * a_part + h) * P:(2 * a_part + h + 1) * P],
                                         W[:, bass.ds(at + (2 * W1PART + w_part * W2PART + h * D), D)],
                                         start=False, stop=(n == 3 * C))
                last.then_inc(y_done, 1)

            starts = [pe.alloc_register(f"weights_at{c}") for c in range(RING)]

            def start_of(c):
                return pe.snap(starts[c % RING], min_val=0, max_val=(E - 1) * WE)

            def step(m, c):
                s = m * RING + c
                if live(s):
                    turn_rows(s, c)
                    pe.load(starts[c], step_at[0:1, bass.ds(s, 1)])
                if live(s - 1):
                    first(s - 1, c - 1, start_of(c - 1))
                if live(s - 3):
                    turn_act(s - 3, c - 3)
                if live(s - 4):
                    second(s - 4, c - 4, start_of(c - 4))

            for c in range(RING):
                step(0, c)
            with pe.Fori(1, ROUNDS) as m:
                for c in range(RING):
                    step(m, c)
            for c in range(4):
                step(ROUNDS, c)

        @block.vector
        def _(dve):
            steps = Steps(dve, dve_step)
            link = steps.link

            dve.wait_ge(consts, 4)
            dve.tensor_copy(ident16[:], ident[:])
            link(dve.memset(count[:], 0.0))
            dve.wait_ge(setup_loaded, 16 * 5)
            link(dve.tensor_scalar(norm_scaled[:], norm[:], W_SCALE, None, ALU.mult))
            link(dve.tensor_reduce(wo_mean[:], wo_raw, AX_X, ALU.add))
            link(dve.tensor_scalar(wo_mean[:], wo_mean[:], -1.0 / D, None, ALU.mult))
            for c in range(C):
                link(dve.tensor_scalar(wos[:, c, :], wo_raw[:, c, :], wo_mean[:, c:c + 1], None, ALU.add))
            dve.wait_ge(setup_turned, 2)
            for h in range(C):
                last = dve.tensor_scalar(gateT[:, h, :], bank[7][:, h * E:(h + 1) * E], norm[:, h:h + 1],
                                         1.0 / U_SCALE, ALU.mult, ALU.mult)
            last.then_inc(setup_done, 1)

            dve.wait_ge(bias_loaded, 16 * 6)
            dve.wait_ge(setup_done, 1)
            b1_out = bias_t[:, 0:O].rearrange("p (c i) -> p c i", c=2)
            b1_in = bias_f[:, 0:O].rearrange("p (i c) -> p c i", c=2)
            link(dve.tensor_scalar(b1_out, b1_in, H_SCALE, None, ALU.mult))
            link(dve.tensor_scalar(bias_t[:, O:O + D], bias_f[:, O:O + D], Y_SCALE, None, ALU.mult))
            link(dve.tensor_copy(bias_rows[:, :], bias_t))
            for n, q in enumerate((32, 64, 64)):
                rest, part_rows = bias_t[q:q + 32, :], bias_rows[q:q + 32, :]
                link(dve.tensor_tensor(rest, rest, part_rows, ALU.subtract))
                dve.tensor_copy(part_rows, rest).then_inc(bias_ready, 1)
                dve.wait_ge(bias_ready, n + 1)

            def moments(source):
                for j in range(TB):
                    last = dve.bn_stats(stats[:, j, :], source(j))
                link(last, apart)
                for j in range(TB):
                    last = dve.bn_aggr(mv[:, j, :], stats[:, j, :])
                link(last)

            def power(value, scalars, n):
                dve.tensor_scalar(var_eps[:], value, scalars[0], scalars[1], ALU.mult,
                                  ALU.add).then_inc(var_ready, 1)
                dve.wait_ge(rstd_ready, n)

            def batch(b):
                dve.wait_ge(x_loaded, 16 * (b + 1))
                apart(dve)
                moments(lambda j: tile_x(b, j))
                power(mv[:, :, 1], (1.0, EPS), 4 * b + 1)
                for j in range(TB):
                    dve.tensor_scalar(XN[:, j, :], tile_x(b, j), mv[:, j, 0:1], rstd[:, j:j + 1], ALU.subtract,
                                      ALU.mult).then_inc(xn_ready, 1)

                dve.wait_ge(scores_done, b + 1)
                link(dve.tensor_reduce(row_max[:], bank[4][:, :].rearrange("p (c d) -> p c d", c=C), AX_X, ALU.max))
                dve.tensor_scalar(row_neg[:], row_max[:], -SCORE_SCALE, None, ALU.mult).then_inc(max_ready, 1)
                dve.wait_ge(exp_done, b + 1)
                link(dve.reciprocal(row_inv[:], row_sum[:]))
                for c in range(C):
                    last = dve.tensor_scalar(probs[:, c, :], probs[:, c, :], row_inv[:, c:c + 1], None, ALU.mult)
                last.then_inc(probs_ready, 1)

                for t in range(TB // 2):
                    dve.wait_ge(att_done, TB // 2 * b + t + 1)
                    for j in (2 * t, 2 * t + 1):
                        last = dve.bn_stats(stats[:, j, :], halves(t)[j % 2])
                link(last, apart)
                for j in range(TB):
                    last = dve.bn_aggr(mv[:, j, :], stats[:, j, :])
                link(last)
                power(mv[:, :, 1], (1.0, EPS), 4 * b + 2)
                for j in range(TB):
                    last = dve.scalar_tensor_tensor(out=tile_x(b, j), in0=halves(j // 2)[j % 2],
                                                    scalar=rstd[:, j:j + 1], in1=tile_x(b, j), op0=ALU.mult,
                                                    op1=ALU.add)
                link(last, apart)

                moments(lambda j: tile_x(b, j))
                power(mv[:, :, 1], (1.0, EPS), 4 * b + 3)
                at = bass.ds(b * TB, TB)
                dve.tensor_copy(ffn_rstd[:, at], rstd[:])
                link(dve.scalar_tensor_tensor(out=ffn_bias[:, at], in0=mv[:, :, 0], scalar=-1.0, in1=rstd[:],
                                              op0=ALU.mult, op1=ALU.mult))
                link(dve.tensor_tensor(mean_sq[:], mv[:, :, 1], rstd[:], ALU.mult))
                link(dve.tensor_tensor(mean_sq[:], mean_sq[:], rstd[:], ALU.mult))
                link(dve.tensor_copy(rms[:], rstd[:]))
                power(mean_sq[:], (1.0, EPS), 4 * b + 4)
                link(dve.scalar_tensor_tensor(out=u_mult[:], in0=rms[:], scalar=U_SCALE, in1=rstd[:],
                                              op0=ALU.mult, op1=ALU.mult))
                for j in range(TB):
                    dve.tensor_scalar(XN[:, j, :], tile_x(b, j), mv[:, j, 0:1], u_mult[:, j:j + 1], ALU.subtract,
                                      ALU.mult).then_inc(u_ready, 1)

                dve.wait_ge(logits_done, TB // 2 * (b + 1))
                link(dve.tensor_tensor(logits[:], bank[5][:, 0:TB * E].rearrange("p (j e) -> p j e", e=E),
                                       gate_b_all[:, :].unsqueeze(1).to_broadcast([P, TB, E]), ALU.add), apart)
                for j in range(TB):
                    last = dve.max(top_v[:, j, :], logits[:, j, :])
                link(last)
                dve.tensor_tensor(gate_e[:], top_v[:, :, 0:TOP], top_v[:, :, 0:1].to_broadcast([P, TB, TOP]),
                                  ALU.subtract).then_inc(gate_in_ready, 1)
                for j in range(TB):
                    last = dve.max_index(top_i[:, j, :], top_v[:, j, :], logits[:, j, :])
                link(last)
                for i in range(2):
                    wait(dve, rows_sent[i], 16 * TOP * (TB // 2) * b)
                link(dve.tensor_copy(top_f[:], top_i[:, :, 0:TOP]))
                top_flat = top_f[:].rearrange("p j k -> p (j k)")
                link(dve.tensor_tensor(onehot[:], top_flat.unsqueeze(2).to_broadcast([P, TB * TOP, E]),
                                       expert_no[:, :].unsqueeze(1).to_broadcast([P, TB * TOP, E]), ALU.is_equal))
                by_expert = onehot[:].rearrange("p (j k) e -> p j e k", k=TOP)
                with nc.allow_low_precision("sums of at most four ones"):
                    dve.tensor_reduce(chosen[:], by_expert, AX_X, ALU.add).then_inc(chosen_ready, 1)
                dve.wait_ge(gate_exp_done, b + 1)
                link(dve.tensor_reduce(gate_sum[:], gate_e[:], AX_X, ALU.add))
                link(dve.reciprocal(gate_inv[:], gate_sum[:]))
                link(dve.scalar_tensor_tensor(out=gates[:], in0=gate_e[:], scalar=1.0 / Y_SCALE,
                                              in1=gate_inv[:, :].unsqueeze(2).to_broadcast([P, TB, TOP]),
                                              op0=ALU.mult, op1=ALU.mult))
                link(dve.tensor_reduce(batch_count[:], onehot[:].rearrange("p t e -> p e t"), AX_X, ALU.add))

                dve.wait_ge(rank_done, b + 1)
                ranks = bank[4][:, 0:TB * E].rearrange("p (j e) -> p j e", e=E)
                for j in range(TB):
                    one = onehot[:, j * TOP:(j + 1) * TOP, :]
                    last = dve.tensor_tensor(one, one, ranks[:, j:j + 1, :].to_broadcast([P, TOP, E]), ALU.mult)
                link(last)
                dve.tensor_tensor(count[:], count[:], batch_count[:], ALU.add).then_inc(counted, 1)
                link(dve.tensor_reduce(rank[:], onehot[:], AX_X, ALU.add))
                link(dve.scalar_tensor_tensor(out=row_f[:], in0=top_flat, scalar=float(REGION), in1=rank[:],
                                              op0=ALU.mult, op1=ALU.add))
                link(dve.tensor_copy(row_i[:], row_f[:]))

                for j in range(TB):
                    dve.wait_ge(hi_staged, TB * b + j + 1)
                    to = stage[:, j % 2]
                    own = to[:, 0, 0:D].bitcast(F16)
                    dve.tensor_tensor(own[:, D:2 * D], XN[:, j, :], own[:, 0:D], ALU.subtract)
                    dve.tensor_copy(to[:, :, PLACE].bitcast(I32), place[:, bass.ds(b * (TB * TOP) + j * TOP, TOP)])
                    link(dve.tensor_copy(to[:, :, GATE], gates[:, j, :]))
                    dve.tensor_copy(to[:, 1:TOP, 0:D].bitcast(F16),
                                    own.unsqueeze(1).to_broadcast([P, TOP - 1, 2 * D])).then_inc(staged, 1)

            start = steps.passed()
            batch(0)
            per_batch = steps.n
            with dve.Fori(1, B) as b:
                steps.base, steps.n = b * per_batch + start, 0
                batch(b)
                assert steps.n == per_batch
            steps.base, steps.n = start + B * per_batch, 0

            dve.wait_ge(counts_done, 1)
            counts = bank[7][:, 0:E]
            link(dve.tensor_tensor(pad_f[:, 0:E], counts[0:1, :], pad_base[:, 0:E], ALU.add))
            link(dve.tensor_copy(pad_f[:, E:E + 1], pad_base[:, E:E + 1]))
            dve.tensor_copy(pad_row[:], pad_f[:]).then_inc(pad_ready, 1)
            link(dve.tensor_scalar(tile_f[:], counts, float(P - 1), None, ALU.add))
            link(dve.tensor_copy(tile_i[:], tile_f[:]))
            link(dve.tensor_scalar(tile_i[:], tile_i[:], P.bit_length() - 1, None, ALU.logical_shift_right))
            link(dve.tensor_copy(cum[:, 0, :], tile_i[:]))
            at, shift = 0, 1
            while shift < E:
                dve.tensor_copy(cum[:, 1 - at, 0:shift], cum[:, at, 0:shift])
                link(dve.tensor_tensor(cum[:, 1 - at, shift:E], cum[:, at, shift:E], cum[:, at, 0:E - shift],
                                       ALU.add))
                at, shift = 1 - at, 2 * shift
            no, step_e, step_t, step_x = (step_f[:, i, :] for i in range(4))
            sums = cum[0:1, at, :].unsqueeze(1).to_broadcast([1, STEPS, E])
            link(dve.tensor_tensor(table, sums, no.unsqueeze(2).to_broadcast([1, STEPS, E]), ALU.is_le))
            link(dve.tensor_reduce(step_e, table, AX_X, ALU.add))
            link(dve.tensor_tensor(table, table, sums, ALU.mult))
            link(dve.tensor_reduce(step_t, table, AX_X, ALU.max))
            link(dve.tensor_tensor(step_t, no, step_t, ALU.subtract))
            link(dve.tensor_scalar(step_x, step_e, float(REGION), None, ALU.mult))
            link(dve.scalar_tensor_tensor(out=step_x, in0=step_t, scalar=float(P), in1=step_x, op0=ALU.mult,
                                          op1=ALU.add))
            link(dve.tensor_scalar(step_x, step_x, float(ROW_MAX), None, ALU.min))
            dve.tensor_copy(step_row[:], step_x)
            link(dve.tensor_scalar(step_e, step_e, float(E - 1), None, ALU.min))
            link(dve.tensor_scalar(step_t, step_e, float(WE), None, ALU.mult))
            dve.tensor_copy(step_at[:], step_t).then_inc(tables_ready, 1)

            def expert(e, r, at):
                for c in range(C):
                    dve.wait_ge(w_high, 3 * e + c + 1)
                    dve.scalar_tensor_tensor(out=W[:, bass.ds(at + W1PART + c * O, O)], in0=bank[3 * r + c][:, :],
                                             scalar=norm_scaled[:, c:c + 1], in1=W[:, bass.ds(at + c * O, O)],
                                             op0=ALU.mult, op1=ALU.subtract).then_inc(w_low, 1)
                dve.wait_ge(w_high, 3 * e + 3)
                dve.scalar_tensor_tensor(out=W[:, bass.ds(at + 2 * W1PART + W2PART, W2PART)],
                                         in0=bank[3 * r + 2][:, :], scalar=W_SCALE,
                                         in1=W[:, bass.ds(at + 2 * W1PART, W2PART)],
                                         op0=ALU.mult, op1=ALU.subtract).then_inc(w_low, 1)

            with dve.Fori(0, E // 2) as k:
                for r in range(2):
                    expert(k * 2 + r, r, k * (2 * WE) + r * WE)

            def step(m, c):
                s = m * RING + c
                if live(s - 2):
                    r = c % 2
                    dve.wait_ge(high_ready, s - 1)
                    dve.tensor_tensor(act_hl[:, r, D:2 * D], act_t[:, r, :], act_hl[:, r, 0:D],
                                      ALU.subtract).then_inc(low_ready, 1)
                if live(s - 1):
                    r = (c - 1) % 2
                    h = bank[2 + r]
                    dve.wait_ge(h_done, s)
                    dve.tensor_scalar(a_t[:, r, :], h[:, 0:D], 1.0 / H_SCALE, LIMIT, ALU.mult,
                                      ALU.min).then_inc(a_ready, 1)
                    dve.tensor_scalar(b_t[:, r, :], h[:, D:2 * D], LIMIT * H_SCALE, -LIMIT * H_SCALE, ALU.min,
                                      ALU.max).then_inc(h_used, 1)
                if live(s - 3):
                    r = (c - 3) % 2
                    dve.wait_ge(act_turned, s - 2)
                    wait(dve, y_done, s - 4)
                    dve.tensor_copy(actT[:, r, :], bank[4 + r][:, :].bitcast(F16)[:, 0:4 * P]).then_inc(act_copied, 1)
                if live(s - 1):
                    r = (c - 1) % 2
                    dve.wait_ge(h_used, s)
                    dve.scalar_tensor_tensor(out=m_t[:, r, :], in0=b_t[:, r, :], scalar=H_SCALE, in1=a_t[:, r, :],
                                             op0=ALU.add, op1=ALU.mult).then_inc(m_ready, 1)
                    dve.wait_ge(sig_ready, s)
                    dve.wait_ge(m_ready, s)
                    dve.scalar_tensor_tensor(out=act_t[:, r, :], in0=m_t[:, r, :], scalar=A_SCALE / H_SCALE,
                                             in1=sig_t[:, r, :], op0=ALU.mult, op1=ALU.mult).then_inc(act_ready, 1)

            for c in range(RING):
                step(0, c)
            with dve.Fori(1, ROUNDS) as m:
                for c in range(RING):
                    step(m, c)
            for c in range(3):
                step(ROUNDS, c)

            def end(b):
                wait(dve, scaled, TB * b)
                for j in range(TB):
                    dve.wait_ge(pairs_added, TB * b + j + 1)
                    dve.tensor_tensor(summed_t[:, j, :], part[:, j, 0:D], part[:, j, D:2 * D],
                                      ALU.add).then_inc(ffn_summed, 1)
                    dve.wait_ge(ffn_in_ready, TB * b + j + 1)
                    dve.wait_ge(ffn_summed, 2 * (TB * b + j) + 1)
                    dve.tensor_tensor(summed_t[:, j, :], summed_t[:, j, :], ffn[:, j, :],
                                      ALU.add).then_inc(ffn_summed, 1)
                    dve.wait_ge(ffn_summed, 2 * (TB * b + j) + 2)
                    last = dve.bn_stats(stats[:, j, :], summed_t[:, j, :])
                link(last, apart)
                for j in range(TB):
                    last = dve.bn_aggr(mv[:, j, :], stats[:, j, :])
                link(last)
                power(mv[:, :, 1], (1.0, EPS), 4 * B + b + 1)
                for j in range(TB):
                    dve.tensor_scalar(summed_t[:, j, :], summed_t[:, j, :], mv[:, j, 0:1], rstd[:, j:j + 1],
                                      ALU.subtract, ALU.mult).then_inc(shifted, 1)
                wait(dve, out_stored, 16 * b)
                for j in range(TB):
                    dve.wait_ge(shifted, TB * b + j + 1)
                    dve.tensor_tensor(fin[:, j, :], summed_t[:, j, :], tile_x(b, j), ALU.add).then_inc(scaled, 1)

            for c in range(RING):
                dve.wait_ge(result_sent[c], 16 * ROUNDS)
            start = steps.passed()
            end(0)
            per_batch = steps.n
            with dve.Fori(1, B) as b:
                steps.base, steps.n = b * per_batch + start, 0
                end(b)


_INS = ["L0_attn_x", "L0_attn_Wq", "L0_attn_Wk", "L0_attn_Wv", "L0_attn_Wo", "L0_ffn_norm_w", "L0_ffn_gate_w",
        "L0_ffn_gate_b", "L0_ffn_w1", "L0_ffn_b1", "L0_ffn_w2", "L0_ffn_b2"]


def kernel(**inputs):
    import numpy as np
    import concourse.bacc as bacc
    from concourse.bass_utils import run_bass_kernel_spmd

    nc = bacc.Bacc("TRN2", target_bir_lowering=False, num_devices=1)
    arrays, args = {}, []
    for name in _INS:
        a = np.ascontiguousarray(inputs[name])
        arrays[f"in_{name}"] = a
        args.append(nc.dram_tensor(f"in_{name}", a.shape, mybir.dt.from_np(a.dtype), kind="ExternalInput").ap())
    out = nc.dram_tensor("out", arrays["in_L0_attn_x"].shape, F32, kind="ExternalOutput").ap()
    moe_block(nc, *args, out)
    r = run_bass_kernel_spmd(nc, [arrays], core_ids=[0])
    return r.results[0]["out"]
```

```python
from contextlib import ExitStack

import concourse.bass as bass
from concourse import mybir

ALU = mybir.AluOpType
ACT = mybir.ActivationFunctionType
AX_X = mybir.AxisListType.X
F32 = mybir.dt.float32
F16 = mybir.dt.float16
BF16 = mybir.dt.bfloat16
I32 = mybir.dt.int32
U32 = mybir.dt.uint32

P = 128
EPS = 1e-5
LIMIT = 7.0
ALPHA = 1.702
TOP = 4
HEADS = 32
U_SCALE = 64.0
W_SCALE = 256.0
A_SCALE = 64.0
H_SCALE = U_SCALE * W_SCALE
Y_SCALE = A_SCALE * W_SCALE


def wait(engine, semaphore, value):
    if not isinstance(value, int) or value > 0:
        engine.wait_ge(semaphore, value)


class Steps:

    def __init__(self, engine, semaphore):
        self.engine, self.semaphore, self.base, self.n = engine, semaphore, 0, 0

    def link(self, instruction, apart=None):
        self.n += 1
        instruction.then_inc(self.semaphore, 1)
        self.engine.wait_ge(self.semaphore, self.base + self.n)
        if apart:
            apart(self.engine)

    def passed(self):
        self.base, self.n = self.base + self.n, 0
        return self.base


def moe_block(nc, x, wq, wk, wv, wo, norm_w, gate_w, gate_b, w1, b1, w2, b2, out):
    B, S, D = x.shape
    E, O, _ = w1.shape
    C = D // P
    assert C == 2 and O == 2 * D and w2.shape == (E, D, D) and S % P == 0
    TB = S // P
    N = B * S
    REGION = N + P
    RING = 8
    STEPS = -(-(N * TOP // P + E - 1) // RING) * RING
    ROUNDS = STEPS // RING
    ROW = D + 2
    PLACE, GATE = D, D + 1
    PAIRS = N * TOP
    W1PART = C * O
    W2PART = C * D
    PICK = 2 * (W1PART + W2PART)
    WE = PICK + P
    SCORE_SCALE = float(D // HEADS) ** -0.5
    ROW_MAX = E * REGION
    FILLS = 3 * (E // B)
    assert FILLS == 12 and TB == 8 and B % 2 == 0

    x_dram = x.rearrange("b (p j) d -> (b p) (j d)", p=P)
    out_dram = out.rearrange("b (p j) d -> (b p) (j d)", p=P)
    rows = nc.dram_tensor("expert_rows", [(E + 1) * REGION, ROW], F32).ap()
    results = nc.dram_tensor("expert_results", [PAIRS, D], F32).ap()
    results_dram = results.rearrange("(q t) d -> q (t d)", t=TB * TOP)

    with ExitStack() as ctx:
        def sb(name, shape, dt=F32):
            return ctx.enter_context(nc.sbuf_tensor(name, shape, dt))

        def sem(name):
            return ctx.enter_context(nc.semaphore(name))

        X = sb("X", [P, B * TB * D])
        W = sb("W", [P, E * WE], F16)
        bias_rows = sb("bias_rows", [96, O + D], BF16)
        ident = sb("ident", [P, P])
        ident16 = sb("ident16", [P, P], F16)
        below = sb("below", [P, P], BF16)
        ones = sb("ones", [P, P], BF16)
        wqs = sb("wqs", [P, C, D])
        wks = sb("wks", [P, C, D])
        wvT = sb("wvT", [P, C, D])
        wos = sb("wos", [P, C, D])
        gateT = sb("gateT", [P, C, E])
        gate_b_all = sb("gate_b_all", [P, E])
        norm = sb("norm", [P, C])
        norm_scaled = sb("norm_scaled", [P, C])
        pow_half = sb("pow_half", [P, TB])
        expert_no = sb("expert_no", [P, E])
        place = sb("place", [P, B * TB * TOP], I32)
        zero_rows = sb("zero_rows", [P, ROW])
        step_at = sb("step_at", [1, STEPS], I32)
        step_row = sb("step_row", [1, STEPS], I32)
        pad_row = sb("pad_row", [1, E + 1], I32)
        ffn_rstd = sb("ffn_rstd", [P, B * TB])
        ffn_bias = sb("ffn_bias", [P, B * TB])
        stats = sb("stats", [P, TB, 6])
        mv = sb("mv", [P, TB, 2])
        var_eps = sb("var_eps", [P, 2, TB])
        rstd_both = sb("rstd_both", [P, 2, TB])
        rstd, rstd_next = rstd_both[:, 0, :], rstd_both[:, 1, :]
        mean_sq = sb("mean_sq", [P, TB])
        rms = sb("rms", [P, TB])
        u_mult = sb("u_mult", [P, TB])
        row_max = sb("row_max", [P, C])
        row_neg = sb("row_neg", [P, C])
        row_sum = sb("row_sum", [P, C])
        row_inv = sb("row_inv", [P, C])
        wo_mean = sb("wo_mean", [P, C])
        logits = sb("logits", [P, TB, E])
        top_v = sb("top_v", [P, TB, 8])
        top_i = sb("top_i", [P, TB, 8], U32)
        top_f = sb("top_f", [P, TB, TOP])
        gate_e = sb("gate_e", [P, TB, TOP])
        gate_sum = sb("gate_sum", [P, TB])
        gate_inv = sb("gate_inv", [P, TB])
        gates = sb("gates", [P, 2, TB, TOP])
        onehot = sb("onehot", [P, TB * TOP, E])
        chosen = sb("chosen", [P, TB, E], BF16)
        batch_count = sb("batch_count", [P, E])
        count = sb("count", [P, E], BF16)
        rank = sb("rank", [P, TB * TOP])
        row_f = sb("row_f", [P, TB * TOP])
        row_i = sb("row_i", [P, 2, TB * TOP], U32)
        x_mean = sb("x_mean", [P, 2, TB])
        x_mean_neg = sb("x_mean_neg", [P, 2, TB])
        squares = sb("squares", [P, 2, TB])
        square_out = sb("square_out", [P, 2, D], BF16)
        stage = sb("stage", [P, 2, TOP, ROW])
        raw1 = sb("raw1", [P, 2, C, O])
        raw2 = sb("raw2", [P, 2, C, D])
        cum = sb("cum", [P, 2, E])
        tile_f = sb("tile_f", [P, E])
        tile_i = sb("tile_i", [P, E], I32)
        step_no = sb("step_no", [1, STEPS])
        pad_f = sb("pad_f", [1, E + 1])
        pad_base = sb("pad_base", [1, E + 1])
        AREA = 4 * TB * D + 2 * D
        area = sb("area", [P, AREA])

        def views(sizes, of=area, dt=F32):
            at, made = 0, []
            for n in sizes:
                made.append(of[:, at:at + n])
                at += n
            assert at <= of.shape[1]
            return made

        turns, xnT, gram, prod, mixer, uT = views([2 * TB * D, C * S, C * D, C * D, C * D, 2 * 512])
        xnT, gram, prod, mixer = (v.rearrange("p (c d) -> p c d", c=C) for v in (xnT, gram, prod, mixer))
        probs = gram
        uT = uT.rearrange("p (r n) -> p r n", r=2)

        def turn_of(side, j):
            return turns[:, side * TB * D + j * D:side * TB * D + (j + 1) * D]

        table = area[0:1, 2 * TB * D:2 * TB * D + STEPS * E].rearrange("p (s e) -> p s e", e=E)
        step_e, step_t, step_x = (
            area[0:1, 2 * TB * D + STEPS * (E + n):2 * TB * D + STEPS * (E + n + 1)] for n in range(3))
        tiles, utp, a_t, b_t, sig_t, m_t, act_t, act_hl, actT, y_t = views(
            [RING * ROW, 2 * D, 2 * D, 2 * D, 2 * D, 2 * D, 2 * D, 2 * D, 2 * D, 4 * D])
        tiles = tiles.rearrange("p (r n) -> p r n", r=RING)
        utp, act_hl, actT = (
            v.bitcast(F16).rearrange("p (r n) -> p r n", r=2) for v in (utp, act_hl, actT))
        a_t, b_t, sig_t, m_t, act_t = (
            v.rearrange("p (r n) -> p r n", r=2) for v in (a_t, b_t, sig_t, m_t, act_t))
        y_t = y_t.rearrange("p (r n) -> p r n", r=4)
        got, part, ffn, summed_t, fin = views(
            [TB * TOP * D, TB * 2 * D, TB * D, TB * D, TB * D], of=W[:, :].bitcast(F32))
        got = got.rearrange("p (j n) -> p j n", j=TB)
        part = part.rearrange("p (j n) -> p j n", j=TB)
        ffn, summed_t, fin = (v.rearrange("p (j d) -> p j d", j=TB) for v in (ffn, summed_t, fin))
        picks = W[0:96, :].bitcast(BF16).rearrange("p (e w) -> p e w", e=E)[:, :, PICK:PICK + P]
        wv_raw = raw2[:, 0]
        gate_raw = raw1[0:E, 0, 0, 0:D]
        wo_raw = raw2[:, 1]
        bias_f = raw1[0:96, 1].rearrange("p c n -> p (c n)")[:, 0:O + D]
        bias_t = raw1[0:96, 0].rearrange("p c n -> p (c n)")[:, 0:O + D]

        bank = [ctx.enter_context(nc.psum_tensor(f"bank{i}", [P, 512], F32)) for i in range(8)]

        x_loaded = sem("x_loaded")
        attn_w_loaded = sem("attn_w_loaded")
        setup_loaded = sem("setup_loaded")
        bias_loaded = sem("bias_loaded")
        raw_loaded = [sem(f"raw_loaded{i}") for i in range(2)]
        rows_sent = [sem(f"rows_sent{i}") for i in range(2)]
        pads_written = sem("pads_written")
        tile_loaded = [sem(f"tile_loaded{i}") for i in range(RING)]
        result_sent = [sem(f"result_sent{i}") for i in range(RING)]
        got_loaded = [sem(f"got_loaded{i}") for i in range(TB)]
        out_stored = sem("out_stored")
        wait_over = sem("wait_over")
        consts = sem("consts")
        pool_first = sem("pool_first")
        bias_zeroed = sem("bias_zeroed")
        setup_turned = sem("setup_turned")
        wv_turned_copied = sem("wv_turned_copied")
        setup_done = sem("setup_done")
        bias_ready = sem("bias_ready")
        dve_step = sem("dve_step")
        var_ready = sem("var_ready")
        rstd_ready = sem("rstd_ready")
        xn_ready = sem("xn_ready")
        gram_done = sem("gram_done")
        gram_copied = sem("gram_copied")
        xn_turned = sem("xn_turned")
        xnT_copied = sem("xnT_copied")
        prod_done = sem("prod_done")
        prod_copied = sem("prod_copied")
        scores_done = sem("scores_done")
        max_ready = sem("max_ready")
        exp_done = sem("exp_done")
        probs_ready = sem("probs_ready")
        mixer_done = sem("mixer_done")
        mixer_copied = sem("mixer_copied")
        att_done = sem("att_done")
        squared = sem("squared")
        x_added = sem("x_added")
        u_ready = sem("u_ready")
        hi_staged = sem("hi_staged")
        u_turned_front = sem("u_turned_front")
        uT_copied_front = sem("uT_copied_front")
        logits_done = sem("logits_done")
        gate_in_ready = sem("gate_in_ready")
        gate_exp_done = sem("gate_exp_done")
        chosen_ready = sem("chosen_ready")
        rank_done = sem("rank_done")
        staged = sem("staged")
        w_turned = sem("w_turned")
        w_high = sem("w_high")
        w_low = sem("w_low")
        counts_done = sem("counts_done")
        counted = sem("counted")
        tables_ready = sem("tables_ready")
        pad_ready = sem("pad_ready")
        u_turned = sem("u_turned")
        u_copied = sem("u_copied")
        h_done = sem("h_done")
        a_ready = sem("a_ready")
        h_used = sem("h_used")
        m_ready = sem("m_ready")
        sig_ready = sem("sig_ready")
        act_ready = sem("act_ready")
        high_ready = sem("high_ready")
        low_ready = sem("low_ready")
        act_turned = sem("act_turned")
        act_copied = sem("act_copied")
        y_done = sem("y_done")
        y_ready = sem("y_ready")
        ffn_in_ready = sem("ffn_in_ready")
        pairs_added = sem("pairs_added")
        ffn_summed = sem("ffn_summed")
        shifted = sem("shifted")
        scaled = sem("scaled")
        got_used = sem("got_used")

        block = ctx.enter_context(nc.Block())

        def tile_x(b, j):
            return X[:, bass.ds(b * (TB * D) + j * D, D)]

        def halves(i):
            return [bank[i][:, 0:D], bank[i][:, D:2 * D]]

        def apart(engine):
            engine.sem_inc(wait_over, 1)

        def live(s):
            return not isinstance(s, int) or 0 <= s < STEPS

        @block.sync
        def _(sp):
            for b in range(B):
                wait(sp, x_loaded, 16 * b)
                sp.dma_start(X[:, b * TB * D:(b + 1) * TB * D], x_dram[b * P:(b + 1) * P, :]).then_inc(x_loaded, 16)
                if b == 0:
                    for w, to in ((wk, wks), (wq, wqs)):
                        sp.dma_start(to[:], w.rearrange("(c p) f -> p c f", p=P)).then_inc(attn_w_loaded, 16)
                    for w, to in ((wv, wv_raw), (wo, wo_raw)):
                        sp.dma_start(to, w.rearrange("(c p) f -> p c f", p=P)).then_inc(setup_loaded, 16)
                    sp.dma_start(gate_raw, gate_w).then_inc(setup_loaded, 16)
                    sp.dma_start(norm[:], norm_w.rearrange("(c p) -> p c", p=P),
                                 allow_slow_non_contiguous=True).then_inc(setup_loaded, 16)
                    sp.dma_start(gate_b_all[:], gate_b.partition_broadcast(P)).then_inc(setup_loaded, 16)
                    sp.wait_ge(bias_zeroed, 1)
                    for part_no in range(3):
                        to = bias_f[32 * part_no:32 * part_no + E, :]
                        sp.dma_start(to[:, 0:O], b1).then_inc(bias_loaded, 16)
                        sp.dma_start(to[:, O:O + D], b2).then_inc(bias_loaded, 16)

            sp.wait_ge(setup_done, 1)
            sp.wait_ge(bias_ready, 3)

            def load_expert(e, r):
                wait(sp, w_low, 3 * (e - 1))
                for q in range(C):
                    w1_e = w1.rearrange("e (r c) h -> (e r) (c h)", c=2)
                    sp.dma_start(raw1[:, r, q, :], w1_e[bass.ds(e * D + q * P, P), :]).then_inc(raw_loaded[r], 16)
                    w2_e = w2.rearrange("e d i -> (e d) i")
                    sp.dma_start(raw2[:, r, q, :], w2_e[bass.ds(e * D + q * P, P), :]).then_inc(raw_loaded[r], 16)

            for r in range(2):
                load_expert(r, r)
            with sp.Fori(1, E // 2) as k:
                for r in range(2):
                    load_expert(k * 2 + r, r)

            sp.wait_ge(pad_ready, 1)
            with sp.Fori(0, E + 1) as e:
                at = sp.value_load(pad_row[0:1, bass.ds(e, 1)], min_val=0, max_val=ROW_MAX)
                sp.dma_start(rows[bass.ds(at, P), :], zero_rows[:]).then_inc(pads_written, 16)
            sp.wait_ge(tables_ready, 1)
            sp.wait_ge(pads_written, 16 * (E + 1))
            for i in range(2):
                sp.wait_ge(rows_sent[i], 16 * TOP * B * TB // 2)

            def load_tile(m, c):
                at = sp.value_load(step_row[0:1, bass.ds(m * RING + c, 1)], min_val=0, max_val=ROW_MAX)
                wait(sp, result_sent[c], 16 * m)
                sp.dma_start(tiles[:, c, :], rows[bass.ds(at, P), :]).then_inc(tile_loaded[c], 16)

            for c in range(RING):
                load_tile(0, c)
            with sp.Fori(1, ROUNDS) as m:
                for c in range(RING):
                    load_tile(m, c)

            for c in range(RING):
                sp.wait_ge(result_sent[c], 16 * ROUNDS)

            def load_results(b, j):
                wait(sp, pairs_added, (b - 1) * TB + j + 1)
                sp.dma_start(got[:, j, :], results_dram[bass.ds(b * P, P), j * TOP * D:(j + 1) * TOP * D]
                             ).then_inc(got_loaded[j], 16)

            def store(b):
                sp.wait_ge(scaled, (b + 1) * TB)
                sp.dma_start(out_dram[bass.ds(b * P, P), :], fin.rearrange("p j d -> p (j d)")).then_inc(out_stored, 16)

            for j in range(TB):
                load_results(0, j)
            with sp.Fori(1, B) as b:
                for j in range(TB):
                    load_results(b, j)
                store(b - 1)
            store(B - 1)
            sp.wait_ge(out_stored, 16 * B)

        @block.gpsimd
        def _(pool):
            pool.memset(raw1[:, 1], 0.0).then_inc(bias_zeroed, 1)
            pool.memset(pow_half[:], -0.5).then_inc(consts, 1)
            pool.memset(ident[:], 0.0).then_inc(pool_first, 1)
            pool.wait_ge(pool_first, 1)
            pool.affine_select(out=ident[:], in_=ident[:], compare_op=ALU.not_equal, fill=1.0, base=0,
                               pattern=[[-1, P]], channel_multiplier=1).then_inc(consts, 1)
            pool.memset(ones[:], 1.0).then_inc(pool_first, 1)
            pool.wait_ge(pool_first, 2)
            pool.affine_select(out=below[:], in_=ones[:], compare_op=ALU.is_gt, fill=0.0, base=0,
                               pattern=[[1, P]], channel_multiplier=-1).then_inc(consts, 1)
            pool.iota(expert_no[:], pattern=[[1, E]], base=0, channel_multiplier=0,
                      allow_small_or_imprecise_dtypes=True).then_inc(consts, 1)
            pool.iota(place[:].rearrange("p (b t) -> p b t", b=B), pattern=[[P * TB * TOP, B], [1, TB * TOP]],
                      base=0, channel_multiplier=TB * TOP).then_inc(consts, 1)
            pool.memset(picks, 0.0).then_inc(pool_first, 1)
            for part_no in range(3):
                pool.wait_ge(pool_first, 3 + part_no)
                pool.affine_select(out=picks, in_=picks, compare_op=ALU.not_equal, fill=1.0, base=-32 * part_no,
                                   pattern=[[-1, E], [0, P]], channel_multiplier=1).then_inc(pool_first, 1)
            pool.memset(zero_rows[:, 0:D], 0.0).then_inc(consts, 1)
            pool.memset(zero_rows[:, GATE:GATE + 1], 0.0).then_inc(consts, 1)
            pool.iota(zero_rows[:, PLACE:PLACE + 1].bitcast(I32), pattern=[[0, 1]], base=PAIRS,
                      channel_multiplier=0).then_inc(consts, 1)
            pool.iota(step_no[:], pattern=[[1, STEPS]], base=0, channel_multiplier=0,
                      allow_small_or_imprecise_dtypes=True).then_inc(consts, 1)
            pool.iota(pad_base[:], pattern=[[REGION, E + 1]], base=0, channel_multiplier=0,
                      allow_small_or_imprecise_dtypes=True).then_inc(consts, 1)

            def power(n, which=0):
                pool.wait_ge(var_ready, n)
                pool.tensor_tensor(rstd_both[:, which, :], var_eps[:, which, :], pow_half[:],
                                   ALU.pow).then_inc(rstd_ready, 1)

            def scatter(b, side, j):
                pool.wait_ge(staged, TB * b + j + 1)
                apart(pool)
                for k in range(TOP):
                    pool.indirect_dma_start(
                        rows, bass.IndirectOffsetOnAxis(ap=row_i[:, side, j * TOP + k:j * TOP + k + 1], axis=0),
                        stage[:, j % 2, k, :], None).then_inc(rows_sent[j % 2], 16)

            def front(i, side, next_batch=True, last_batch=True):
                if last_batch:
                    scatter(i - 1, 1 - side, 2)
                power(4 * i + 3)
                if last_batch:
                    scatter(i - 1, 1 - side, 3)
                power(4 * i + 4)
                power(4 * i + 5)
                if last_batch:
                    for j in range(4, 7):
                        scatter(i - 1, 1 - side, j)
                if next_batch:
                    power(4 * i + 6, 1)
                if last_batch:
                    scatter(i - 1, 1 - side, 7)
                for j in range(2):
                    scatter(i, side, j)

            power(1, 1)
            power(2, 1)
            front(0, 0, last_batch=False)
            with pool.Fori(0, (B - 2) // 2) as k:
                front(2 * k + 1, 1)
                front(2 * k + 2, 0)
            front(B - 1, (B - 1) % 2, next_batch=False)
            for j in range(2, TB):
                scatter(B - 1, (B - 1) % 2, j)

            def send(m, c):
                pool.wait_ge(y_ready, m * RING + c + 1)
                apart(pool)
                pool.indirect_dma_start(
                    results, bass.IndirectOffsetOnAxis(ap=tiles[:, c, PLACE:PLACE + 1].bitcast(U32), axis=0),
                    y_t[:, c % 4, :], None, bounds_check=last_place, oob_is_err=False).then_inc(result_sent[c], 16)

            last_place = pool.to_reg(PAIRS - 1)
            with pool.Fori(0, ROUNDS) as m:
                for c in range(RING):
                    send(m, c)

            def end(b):
                for j in range(TB):
                    pool.wait_ge(got_loaded[j], 16 * (b + 1))
                    wait(pool, ffn_summed, 2 * ((b - 1) * TB + j + 1))
                    pool.tensor_tensor(part[:, j, :], got[:, j, 0:2 * D], got[:, j, 2 * D:4 * D],
                                       ALU.add).then_inc(pairs_added, 1)
                power(4 * B + b + 2)

            end(0)
            with pool.Fori(1, B) as b:
                end(b)

        @block.scalar
        def _(act):
            def copy(to, of):
                return act.activation(to, of, ACT.Copy)

            act.wait_ge(setup_turned, 1)
            copy(wvT[:].rearrange("p c d -> p (c d)"), bank[6][:, :]).then_inc(wv_turned_copied, 1)

            def gram_out(b):
                act.wait_ge(gram_done, b + 1)
                copy(gram.rearrange("p c d -> p (c d)"), bank[4][:, :]).then_inc(gram_copied, 1)

            def turned_out(b, t):
                act.wait_ge(xn_turned, TB // 2 * b + t + 1)
                wait(act, att_done, TB // 2 * b)
                copy(xnT[:, :, t * 2 * P:(t + 1) * 2 * P],
                     bank[6 + t % 2][:, :].rearrange("p (c n) -> p c n", c=C)).then_inc(xnT_copied, 1)

            def prod_out(n):
                act.wait_ge(prod_done, n)
                copy(prod.rearrange("p c d -> p (c d)"), bank[5][:, :]).then_inc(prod_copied, 1)

            def exp_scores(b):
                act.wait_ge(max_ready, b + 1)
                for c in range(C):
                    last = act.activation(probs[:, c, :], halves(4)[c], ACT.Exp, bias=row_neg[:, c:c + 1],
                                          scale=SCORE_SCALE, accum_out=row_sum[:, c:c + 1])
                last.then_inc(exp_done, 1)

            def mixer_out(b):
                act.wait_ge(mixer_done, b + 1)
                wait(act, att_done, TB // 2 * b)
                copy(mixer.rearrange("p c d -> p (c d)"), bank[4][:, :]).then_inc(mixer_copied, 1)

            def u_out(b, t):
                act.wait_ge(u_turned_front, TB // 2 * b + t + 1)
                wait(act, logits_done, TB // 2 * b + t - 1)
                copy(uT[:, t % 2, :], bank[2 + t % 2][:, :]).then_inc(uT_copied_front, 1)

            def high_rows(b, side, j):
                act.wait_ge(u_ready, TB * b + j + 1)
                wait(act, rows_sent[j % 2], 16 * TOP * (TB // 2 * b + j // 2))
                copy(stage[:, j % 2, 0, 0:P].bitcast(F16), turn_of(side, j)).then_inc(hi_staged, 1)

            def high_weights(i, n):
                part_no, at = n % 3, i * (4 * WE) + n // 3 * WE
                act.wait_ge(w_turned, FILLS * i + n + 1)
                if part_no < C:
                    to, scale = W[:, bass.ds(at + part_no * O, O)], norm_scaled[:, part_no:part_no + 1]
                else:
                    to, scale = W[:, bass.ds(at + 2 * W1PART, W2PART)], W_SCALE
                act.activation(to, bank[6 + n % 2][:, :], ACT.Copy, scale=scale).then_inc(w_high, 1)

            def square(b, side, n):
                which, j = divmod(n, TB)
                if which == 0:
                    if j % 2 == 0:
                        act.wait_ge(att_done, TB // 2 * b + j // 2 + 1)
                    of, less = halves(j // 2)[j % 2], 0.0
                else:
                    act.wait_ge(x_added, TB * b + j + 1)
                    of, less = tile_x(b, j), x_mean_neg[:, 1 - side, j:j + 1]
                wait(act, squared, 2 * TB * b + n - 1)
                act.activation(square_out[:, n % 2, :], of, ACT.Square, bias=less,
                               accum_out=squares[:, which, j:j + 1]).then_inc(squared, 1)

            def front(i, side, next_batch=True, last_batch=True):
                def staging(j):
                    if last_batch:
                        high_rows(i - 1, 1 - side, j)

                high_weights(i, 0)
                high_weights(i, 1)
                staging(2)
                for j in range(TB):
                    square(i, side, j)
                staging(3)
                high_weights(i, 2)
                high_weights(i, 3)
                for j in range(TB):
                    square(i, side, TB + j)
                staging(4)
                if next_batch:
                    gram_out(i + 1)
                    for t in range(TB // 2):
                        turned_out(i + 1, t)
                    prod_out(2 * i + 3)
                staging(5)
                u_out(i, 0)
                u_out(i, 1)
                if next_batch:
                    exp_scores(i + 1)
                u_out(i, 2)
                u_out(i, 3)
                staging(6)
                high_weights(i, 4)
                high_weights(i, 5)
                staging(7)
                if next_batch:
                    prod_out(2 * i + 4)
                act.wait_ge(gate_in_ready, i + 1)
                act.activation(gate_e[:], gate_e[:], ACT.Exp).then_inc(gate_exp_done, 1)
                if next_batch:
                    mixer_out(i + 1)
                high_weights(i, 6)
                high_weights(i, 7)
                high_rows(i, side, 0)
                high_weights(i, 8)
                high_rows(i, side, 1)
                for n in range(9, FILLS):
                    high_weights(i, n)

            gram_out(0)
            for t in range(TB // 2):
                turned_out(0, t)
            prod_out(1)
            exp_scores(0)
            prod_out(2)
            mixer_out(0)
            front(0, 0, last_batch=False)
            with act.Fori(0, (B - 2) // 2) as k:
                front(2 * k + 1, 1)
                front(2 * k + 2, 0)
            front(B - 1, (B - 1) % 2, next_batch=False)
            for j in range(2, TB):
                high_rows(B - 1, (B - 1) % 2, j)

            def step(m, c):
                s = m * RING + c
                if live(s):
                    act.wait_ge(u_turned, s + 1)
                    wait(act, h_done, s - 1)
                    act.copy(utp[:, c % 2, :], bank[c % 2][:, :].bitcast(F16)[:, 0:4 * P]).then_inc(u_copied, 1)
                if live(s - 2):
                    act.wait_ge(act_ready, s - 1)
                    wait(act, act_turned, s - 3)
                    copy(act_hl[:, c % 2, 0:D], act_t[:, c % 2, :]).then_inc(high_ready, 1)
                if live(s - 1):
                    act.wait_ge(a_ready, s)
                    act.activation(sig_t[:, (c - 1) % 2, :], a_t[:, (c - 1) % 2, :], ACT.Sigmoid,
                                   scale=ALPHA).then_inc(sig_ready, 1)
                if live(s - 5):
                    act.wait_ge(y_done, s - 4)
                    q, slot = divmod(c - 9, RING)
                    wait(act, result_sent[slot], 16 * (m + q + 1))
                    act.activation(y_t[:, (c - 5) % 4, :], bank[6 + (c - 5) % 2][:, 0:D], ACT.Copy,
                                   scale=tiles[:, (c - 5) % RING, GATE:GATE + 1]).then_inc(y_ready, 1)

            for c in range(RING):
                step(0, c)
            with act.Fori(1, ROUNDS) as m:
                for c in range(RING):
                    step(m, c)
            for c in range(5):
                step(ROUNDS, c)

            for c in range(RING):
                act.wait_ge(result_sent[c], 16 * ROUNDS)

            def end(b):
                for j in range(TB):
                    wait(act, ffn_summed, 2 * ((b - 1) * TB + j + 1))
                    act.activation(ffn[:, j, :], tile_x(b, j), ACT.Identity,
                                   scale=ffn_rstd[:, bass.ds(b * TB + j, 1)],
                                   bias=ffn_bias[:, bass.ds(b * TB + j, 1)]).then_inc(ffn_in_ready, 1)

            end(0)
            with act.Fori(1, B) as b:
                end(b)

        @block.tensor
        def _(pe):
            pe.wait_ge(consts, 2)
            pe.wait_ge(setup_loaded, 16 * 5)
            for f in range(C):
                for h in range(C):
                    last = pe.transpose(bank[6][:, f * D + h * P:f * D + (h + 1) * P],
                                        wv_raw[:, h, f * P:(f + 1) * P], ident[:, :])
            last.then_inc(setup_turned, 1)
            for h in range(C):
                last = pe.transpose(bank[7][:, h * E:(h + 1) * E], gate_raw[:, h * P:(h + 1) * P],
                                    ident[0:E, 0:E])
            last.then_inc(setup_turned, 1)
            pe.wait_ge(wv_turned_copied, 1)
            pe.wait_ge(setup_done, 1)
            pe.wait_ge(attn_w_loaded, 32)

            def square(to, left, right):
                for m in range(C):
                    for c in range(C):
                        last = pe.matmul(halves(to)[m], left[:, c, m * P:(m + 1) * P], right[:, c, :],
                                         start=(c == 0), stop=(c == C - 1))
                return last

            def gram_of(b, side):
                pe.wait_ge(xn_ready, TB * (b + 1))
                for h in range(C):
                    for j in range(TB):
                        last = pe.matmul(halves(4)[h], turn_of(side, j)[:, h * P:(h + 1) * P], turn_of(side, j),
                                         start=(j == 0), stop=(j == TB - 1))
                last.then_inc(gram_done, 1)
                for t in range(TB // 2):
                    if t < 2:
                        wait(pe, w_low, FILLS * (b - 1) + 3 + t)
                    else:
                        wait(pe, xnT_copied, TB // 2 * b + t - 1)
                    for c in range(C):
                        for j in range(2):
                            last = pe.transpose(bank[6 + t % 2][:, (2 * c + j) * P:(2 * c + j + 1) * P],
                                                turn_of(side, 2 * t + j)[:, c * P:(c + 1) * P], ident[:, :])
                    last.then_inc(xn_turned, 1)

            def scores_of(b):
                pe.wait_ge(gram_copied, b + 1)
                square(5, gram, wks).then_inc(prod_done, 1)
                pe.wait_ge(prod_copied, 2 * b + 1)
                square(4, wqs, prod).then_inc(scores_done, 1)

            def mixer_of(b):
                pe.wait_ge(probs_ready, b + 1)
                square(5, probs, wos).then_inc(prod_done, 1)
                pe.wait_ge(prod_copied, 2 * b + 2)
                square(4, wvT, prod).then_inc(mixer_done, 1)

            def attend(b):
                pe.wait_ge(mixer_copied, b + 1)
                pe.wait_ge(xnT_copied, TB // 2 * (b + 1))
                wait(pe, counted, b)
                for j in range(TB):
                    for c in range(C):
                        last = pe.matmul(halves(j // 2)[j % 2], xnT[:, c, j * P:(j + 1) * P], mixer[:, c, :],
                                         start=(c == 0), stop=(c == C - 1))
                    if j % 2:
                        last.then_inc(att_done, 1)

            def logits_of(b, side):
                def turn(t):
                    pe.wait_ge(u_ready, TB * b + 2 * t + 2)
                    wait(pe, uT_copied_front, TB // 2 * b + t - 1)
                    for j in range(2):
                        for c in range(C):
                            last = pe.transpose(bank[2 + t % 2][:, (2 * j + c) * P:(2 * j + c + 1) * P],
                                                turn_of(side, 2 * t + j)[:, c * P:(c + 1) * P], ident[:, :])
                    last.then_inc(u_turned_front, 1)

                def route(t):
                    pe.wait_ge(uT_copied_front, TB // 2 * b + t + 1)
                    for j in range(2):
                        for c in range(C):
                            last = pe.matmul(bank[0][:, (2 * t + j) * E:(2 * t + j + 1) * E],
                                             uT[:, t % 2, (2 * j + c) * P:(2 * j + c + 1) * P], gateT[:, c, :],
                                             start=(c == 0), stop=(c == C - 1))
                    last.then_inc(logits_done, 1)

                turn(0)
                for t in range(1, TB // 2):
                    turn(t)
                    route(t - 1)
                route(TB // 2 - 1)

            def ranks_of(b):
                pe.wait_ge(chosen_ready, b + 1)
                ranks = bank[1][:, 0:TB * E].rearrange("p (j e) -> p j e", e=E)
                pe.matmul(ranks, below[:, :], chosen[:, :, :], start=True, stop=False)
                for j in range(TB - 1):
                    pe.matmul(ranks[:, j + 1:TB, :], ones[:, :],
                              chosen[:, j:j + 1, :].to_broadcast([P, TB - 1 - j, E]), start=False, stop=False,
                              skip_group_check=True)
                pe.matmul(ranks, ones[:, :], count[:, :].unsqueeze(1).to_broadcast([P, TB, E]),
                          start=False, stop=True).then_inc(rank_done, 1)

            def turn_weights(i, n):
                part_no, r = n % 3, n // 3 % 2
                if part_no == 0:
                    pe.wait_ge(raw_loaded[r], i * 128 + n // 6 * 64 + 64)
                wait(pe, w_low, FILLS * i + n - 1)
                if n in (0, 4):
                    pe.wait_ge(xnT_copied, TB // 2 * (i + 1 if n == 0 or isinstance(i, int) and i == B - 1 else i + 2))
                to = bank[6 + n % 2]
                for c in range(2):
                    for q in range(C):
                        if part_no < C:
                            of = raw1[:, r, q, c * D + part_no * P:c * D + (part_no + 1) * P]
                        else:
                            of = raw2[:, r, q, c * P:(c + 1) * P]
                        last = pe.transpose(to[:, c * D + q * P:c * D + (q + 1) * P], of, ident[:, :])
                last.then_inc(w_turned, 1)

            def front(i, side, next_batch=True):
                turn_weights(i, 0)
                turn_weights(i, 1)
                attend(i)
                turn_weights(i, 2)
                turn_weights(i, 3)
                if next_batch:
                    gram_of(i + 1, side)
                    scores_of(i + 1)
                logits_of(i, side)
                turn_weights(i, 4)
                turn_weights(i, 5)
                if next_batch:
                    mixer_of(i + 1)
                ranks_of(i)
                for n in range(6, FILLS):
                    turn_weights(i, n)

            gram_of(0, 1)
            scores_of(0)
            mixer_of(0)
            front(0, 0)
            with pe.Fori(0, (B - 2) // 2) as k:
                front(2 * k + 1, 1)
                front(2 * k + 2, 0)
            front(B - 1, (B - 1) % 2, next_batch=False)

            pe.wait_ge(counted, B)
            pe.matmul(bank[5][:, 0:E], ones[:, :], count[:, :], start=True, stop=True).then_inc(counts_done, 1)

            pe.wait_ge(tables_ready, 1)
            pe.wait_ge(w_low, 3 * E)
            pe.wait_ge(bias_ready, 3)

            def turn_rows(s, c):
                pe.wait_ge(tile_loaded[c % RING], 16 * (s // RING + 1) if isinstance(s, int) else (s - c) * 2 + 16)
                wait(pe, u_copied, s - 1)
                of = tiles[:, c % RING, 0:D].bitcast(F16)
                to = bank[c % 2][:, :].bitcast(F16)
                for k in range(4):
                    last = pe.transpose(to[:, k * P:(k + 1) * P], of[:, k * P:(k + 1) * P], ident16[:, :])
                last.then_inc(u_turned, 1)

            def first(s, c, at):
                pe.wait_ge(u_copied, s + 1)
                wait(pe, h_used, s - 1)
                to = bank[2 + c % 2][:, :]
                pe.matmul(to, W[0:96, bass.ds(at + PICK, P)].bitcast(BF16), bias_rows[:, 0:O], start=True, stop=False)
                n = 0
                for h in range(C):
                    for u_part, w_part in ((0, 0), (1, 0), (0, 1)):
                        n += 1
                        last = pe.matmul(to, utp[:, c % 2, (2 * u_part + h) * P:(2 * u_part + h + 1) * P],
                                         W[:, bass.ds(at + (w_part * W1PART + h * O), O)],
                                         start=False, stop=(n == 3 * C))
                last.then_inc(h_done, 1)

            def turn_act(s, c):
                pe.wait_ge(low_ready, s + 1)
                wait(pe, act_copied, s - 1)
                to = bank[4 + c % 2][:, :].bitcast(F16)
                for k in range(4):
                    last = pe.transpose(to[:, k * P:(k + 1) * P], act_hl[:, c % 2, k * P:(k + 1) * P], ident16[:, :])
                last.then_inc(act_turned, 1)

            def second(s, c, at):
                pe.wait_ge(act_copied, s + 1)
                wait(pe, y_ready, s - 1)
                to = bank[6 + c % 2][:, 0:D]
                pe.matmul(to, W[0:96, bass.ds(at + PICK, P)].bitcast(BF16), bias_rows[:, O:O + D],
                          start=True, stop=False)
                n = 0
                for h in range(C):
                    for a_part, w_part in ((0, 0), (1, 0), (0, 1)):
                        n += 1
                        last = pe.matmul(to, actT[:, c % 2, (2 * a_part + h) * P:(2 * a_part + h + 1) * P],
                                         W[:, bass.ds(at + (2 * W1PART + w_part * W2PART + h * D), D)],
                                         start=False, stop=(n == 3 * C))
                last.then_inc(y_done, 1)

            starts = [pe.alloc_register(f"weights_at{c}") for c in range(RING)]

            def start_of(c):
                return pe.snap(starts[c % RING], min_val=0, max_val=(E - 1) * WE)

            def step(m, c):
                s = m * RING + c
                if live(s):
                    turn_rows(s, c)
                if live(s - 1):
                    first(s - 1, c - 1, start_of(c - 1))
                if live(s):
                    pe.load(starts[c], step_at[0:1, bass.ds(s, 1)])
                if live(s - 3):
                    turn_act(s - 3, c - 3)
                if live(s - 4):
                    second(s - 4, c - 4, start_of(c - 4))

            for c in range(RING):
                step(0, c)
            with pe.Fori(1, ROUNDS) as m:
                for c in range(RING):
                    step(m, c)
            for c in range(4):
                step(ROUNDS, c)

        @block.vector
        def _(dve):
            steps = Steps(dve, dve_step)
            link = steps.link

            dve.wait_ge(consts, 4)
            dve.tensor_copy(ident16[:], ident[:])
            link(dve.memset(count[:], 0.0))
            dve.wait_ge(setup_loaded, 16 * 5)
            link(dve.tensor_scalar(norm_scaled[:], norm[:], W_SCALE, None, ALU.mult))
            link(dve.tensor_reduce(wo_mean[:], wo_raw, AX_X, ALU.add))
            link(dve.tensor_scalar(wo_mean[:], wo_mean[:], -1.0 / D, None, ALU.mult))
            for c in range(C):
                link(dve.tensor_scalar(wos[:, c, :], wo_raw[:, c, :], wo_mean[:, c:c + 1], None, ALU.add))
            dve.wait_ge(setup_turned, 2)
            for h in range(C):
                last = dve.tensor_scalar(gateT[:, h, :], bank[7][:, h * E:(h + 1) * E], norm[:, h:h + 1],
                                         1.0 / U_SCALE, ALU.mult, ALU.mult)
            last.then_inc(setup_done, 1)

            def moments(source):
                for j in range(TB):
                    last = dve.bn_stats(stats[:, j, :], source(j))
                link(last, apart)
                for j in range(TB):
                    last = dve.bn_aggr(mv[:, j, :], stats[:, j, :])
                link(last)

            def split_biases():
                dve.wait_ge(bias_loaded, 16 * 6)
                dve.wait_ge(setup_done, 1)
                b1_out = bias_t[:, 0:O].rearrange("p (c i) -> p c i", c=2)
                b1_in = bias_f[:, 0:O].rearrange("p (i c) -> p c i", c=2)
                link(dve.tensor_scalar(b1_out, b1_in, H_SCALE, None, ALU.mult))
                link(dve.tensor_scalar(bias_t[:, O:O + D], bias_f[:, O:O + D], Y_SCALE, None, ALU.mult))
                link(dve.tensor_copy(bias_rows[:, :], bias_t))
                for n, q in enumerate((32, 64, 64)):
                    rest, part_rows = bias_t[q:q + 32, :], bias_rows[q:q + 32, :]
                    link(dve.tensor_tensor(rest, rest, part_rows, ALU.subtract))
                    dve.tensor_copy(part_rows, rest).then_inc(bias_ready, 1)
                    dve.wait_ge(bias_ready, n + 1)

            def nothing():
                pass

            def ask_power(value, scale, which=0):
                dve.tensor_scalar(var_eps[:, which, :], value, scale, EPS, ALU.mult, ALU.add).then_inc(var_ready, 1)

            def power(value, scale, n, meanwhile=nothing):
                ask_power(value, scale)
                meanwhile()
                dve.wait_ge(rstd_ready, n)

            def norm_stats(b, side):
                moments(lambda j: tile_x(b, j))
                dve.tensor_copy(x_mean[:, side, :], mv[:, :, 0])
                dve.tensor_scalar(x_mean_neg[:, side, :], mv[:, :, 0], -1.0, None, ALU.mult)
                ask_power(mv[:, :, 1], 1.0, 1)

            def norm_of(b, side, n):
                dve.wait_ge(rstd_ready, n)
                for j in range(TB):
                    dve.tensor_scalar(turn_of(side, j), tile_x(b, j), mv[:, j, 0:1], rstd_next[:, j:j + 1],
                                      ALU.subtract, ALU.mult).then_inc(xn_ready, 1)

            def softmax_of(b, before=nothing, meanwhile=nothing):
                dve.wait_ge(scores_done, b + 1)
                link(dve.tensor_reduce(row_max[:], bank[4][:, :].rearrange("p (c d) -> p c d", c=C), AX_X, ALU.max))
                dve.tensor_scalar(row_neg[:], row_max[:], -SCORE_SCALE, None, ALU.mult).then_inc(max_ready, 1)
                meanwhile()
                dve.wait_ge(exp_done, b + 1)
                link(dve.reciprocal(row_inv[:], row_sum[:]))
                for c in range(C):
                    last = dve.tensor_scalar(probs[:, c, :], probs[:, c, :], row_inv[:, c:c + 1], None, ALU.mult)
                last.then_inc(probs_ready, 1)

            def attention_added(b, n, meanwhile):
                dve.wait_ge(squared, 2 * TB * b + TB)
                power(squares[:, 0, :], 1.0 / D, n, meanwhile=meanwhile)
                for j in range(TB):
                    dve.scalar_tensor_tensor(out=tile_x(b, j), in0=halves(j // 2)[j % 2], scalar=rstd[:, j:j + 1],
                                             in1=tile_x(b, j), op0=ALU.mult, op1=ALU.add).then_inc(x_added, 1)

            def u_of(b, side, n, next_batch, meanwhile, meanwhile_2):
                dve.wait_ge(squared, 2 * TB * (b + 1))
                power(squares[:, 1, :], 1.0 / D, n, meanwhile=meanwhile)
                at = bass.ds(b * TB, TB)
                dve.tensor_copy(ffn_rstd[:, at], rstd)
                dve.tensor_tensor(ffn_bias[:, at], x_mean_neg[:, 1 - side, :], rstd, ALU.mult)
                link(dve.tensor_tensor(mean_sq[:], squares[:, 1, :], rstd, ALU.mult))
                link(dve.tensor_tensor(mean_sq[:], mean_sq[:], rstd, ALU.mult))
                link(dve.tensor_copy(rms[:], rstd))
                power(mean_sq[:], 1.0 / D, n + 1, meanwhile=meanwhile_2)
                link(dve.scalar_tensor_tensor(out=u_mult[:], in0=rms[:], scalar=U_SCALE, in1=rstd,
                                              op0=ALU.mult, op1=ALU.mult))
                if next_batch:
                    dve.wait_ge(xn_turned, TB // 2 * (b + 2))
                for j in range(TB):
                    dve.tensor_scalar(turn_of(side, j), tile_x(b, j), x_mean[:, 1 - side, j:j + 1], u_mult[:, j:j + 1],
                                      ALU.subtract, ALU.mult).then_inc(u_ready, 1)

            top_flat = top_f[:].rearrange("p j k -> p (j k)")

            def choose(b, meanwhile):
                dve.wait_ge(logits_done, TB // 2 * (b + 1))
                link(dve.tensor_tensor(logits[:], bank[0][:, 0:TB * E].rearrange("p (j e) -> p j e", e=E),
                                       gate_b_all[:, :].unsqueeze(1).to_broadcast([P, TB, E]), ALU.add), apart)
                for j in range(TB):
                    last = dve.max(top_v[:, j, :], logits[:, j, :])
                link(last)
                dve.tensor_tensor(gate_e[:], top_v[:, :, 0:TOP], top_v[:, :, 0:1].to_broadcast([P, TB, TOP]),
                                  ALU.subtract).then_inc(gate_in_ready, 1)
                for j in range(TB):
                    last = dve.max_index(top_i[:, j, :], top_v[:, j, :], logits[:, j, :])
                link(last)
                link(dve.tensor_copy(top_f[:], top_i[:, :, 0:TOP]))
                link(dve.tensor_tensor(onehot[:], top_flat.unsqueeze(2).to_broadcast([P, TB * TOP, E]),
                                       expert_no[:, :].unsqueeze(1).to_broadcast([P, TB * TOP, E]), ALU.is_equal))
                by_expert = onehot[:].rearrange("p (j k) e -> p j e k", k=TOP)
                with nc.allow_low_precision("sums of at most four ones"):
                    dve.tensor_reduce(chosen[:], by_expert, AX_X, ALU.add).then_inc(chosen_ready, 1)
                link(dve.tensor_reduce(batch_count[:], onehot[:].rearrange("p t e -> p e t"), AX_X, ALU.add))
                meanwhile()

            def gates_of(b, side):
                dve.wait_ge(gate_exp_done, b + 1)
                link(dve.tensor_reduce(gate_sum[:], gate_e[:], AX_X, ALU.add))
                link(dve.reciprocal(gate_inv[:], gate_sum[:]))
                link(dve.scalar_tensor_tensor(out=gates[:, side, :, :], in0=gate_e[:], scalar=1.0 / Y_SCALE,
                                              in1=gate_inv[:, :].unsqueeze(2).to_broadcast([P, TB, TOP]),
                                              op0=ALU.mult, op1=ALU.mult))

            def places_of(b, side):
                dve.wait_ge(rank_done, b + 1)
                ranks = bank[1][:, 0:TB * E].rearrange("p (j e) -> p j e", e=E)
                for j in range(TB):
                    one = onehot[:, j * TOP:(j + 1) * TOP, :]
                    last = dve.tensor_tensor(one, one, ranks[:, j:j + 1, :].to_broadcast([P, TOP, E]), ALU.mult)
                link(last)
                dve.tensor_tensor(count[:], count[:], batch_count[:], ALU.add).then_inc(counted, 1)
                link(dve.tensor_reduce(rank[:], onehot[:], AX_X, ALU.add))
                link(dve.scalar_tensor_tensor(out=row_f[:], in0=top_flat, scalar=float(REGION), in1=rank[:],
                                              op0=ALU.mult, op1=ALU.add))
                link(dve.tensor_copy(row_i[:, side, :], row_f[:]))

            def stage_rows(b, side, j):
                dve.wait_ge(hi_staged, TB * b + j + 1)
                to = stage[:, j % 2]
                own = to[:, 0, 0:D].bitcast(F16)
                dve.tensor_tensor(own[:, D:2 * D], turn_of(side, j), own[:, 0:D], ALU.subtract)
                dve.tensor_copy(to[:, :, PLACE].bitcast(I32), place[:, bass.ds(b * (TB * TOP) + j * TOP, TOP)])
                link(dve.tensor_copy(to[:, :, GATE], gates[:, side, j, :]))
                dve.tensor_copy(to[:, 1:TOP, 0:D].bitcast(F16),
                                own.unsqueeze(1).to_broadcast([P, TOP - 1, 2 * D])).then_inc(staged, 1)

            def low_weights(i, n):
                part_no, at = n % 3, i * (4 * WE) + n // 3 * WE
                dve.wait_ge(w_high, FILLS * i + n + 1)
                if part_no < C:
                    high, low = (W[:, bass.ds(at + k * W1PART + part_no * O, O)] for k in range(2))
                    scale = norm_scaled[:, part_no:part_no + 1]
                else:
                    high, low = (W[:, bass.ds(at + 2 * W1PART + k * W2PART, W2PART)] for k in range(2))
                    scale = W_SCALE
                dve.scalar_tensor_tensor(out=low, in0=bank[6 + n % 2][:, :], scalar=scale, in1=high,
                                         op0=ALU.mult, op1=ALU.subtract).then_inc(w_low, 1)

            def front(i, side, next_batch=True, last_batch=True):
                def fill(rows_of=None, weights_of=()):
                    if last_batch and rows_of is not None:
                        stage_rows(i - 1, 1 - side, rows_of)
                    for n in weights_of:
                        low_weights(i, n)

                if next_batch:
                    norm_of(i + 1, side, 4 * i + 2)
                fill(2, (0, 1))
                attention_added(i, 4 * i + 3, lambda: fill(3, (2, 3)))
                u_of(i, side, 4 * i + 4, next_batch, nothing, lambda: fill(4))
                fill(5)
                if next_batch:
                    softmax_of(i + 1, meanwhile=lambda: norm_stats((i + 2) % B, 1 - side))
                fill(6)
                choose(i, lambda: fill(7, (4, 5)))
                gates_of(i, side)
                places_of(i, side)
                fill(None, (6,))
                stage_rows(i, side, 0)
                fill(None, (7, 8))
                stage_rows(i, side, 1)
                fill(None, range(9, FILLS))

            for b in range(2):
                dve.wait_ge(x_loaded, 16 * (b + 1))
                norm_stats(b, 1 - b)
                if b == 0:
                    norm_of(0, 1, 1)
            dve.wait_ge(x_loaded, 16 * B)
            split_biases()
            softmax_of(0)
            before = steps.n
            front(0, 0, last_batch=False)
            per_batch = steps.n - before + TB - 2
            start = steps.passed()
            with dve.Fori(0, (B - 2) // 2) as k:
                steps.base, steps.n = k * (2 * per_batch) + start, 0
                front(2 * k + 1, 1)
                front(2 * k + 2, 0)
                assert steps.n == 2 * per_batch
            steps.base, steps.n = start + (B - 2) * per_batch, 0
            front(B - 1, (B - 1) % 2, next_batch=False)

            def paddings():
                dve.wait_ge(counts_done, 1)
                link(dve.tensor_tensor(pad_f[:, 0:E], counts[0:1, :], pad_base[:, 0:E], ALU.add))
                link(dve.tensor_copy(pad_f[:, E:E + 1], pad_base[:, E:E + 1]))
                dve.tensor_copy(pad_row[:], pad_f[:]).then_inc(pad_ready, 1)

            def tile_sums():
                link(dve.tensor_scalar(tile_f[:], counts, float(P - 1), None, ALU.add))
                link(dve.tensor_copy(tile_i[:], tile_f[:]))
                link(dve.tensor_scalar(tile_i[:], tile_i[:], P.bit_length() - 1, None, ALU.logical_shift_right))
                link(dve.tensor_copy(cum[:, 0, :], tile_i[:]))
                at, shift = 0, 1
                while shift < E:
                    dve.tensor_copy(cum[:, 1 - at, 0:shift], cum[:, at, 0:shift])
                    link(dve.tensor_tensor(cum[:, 1 - at, shift:E], cum[:, at, shift:E], cum[:, at, 0:E - shift],
                                           ALU.add))
                    at, shift = 1 - at, 2 * shift
                return cum[0:1, at, :].unsqueeze(1).to_broadcast([1, STEPS, E])

            def step_experts(sums):
                link(dve.tensor_tensor(table, sums, no.unsqueeze(2).to_broadcast([1, STEPS, E]), ALU.is_le))
                link(dve.tensor_reduce(step_e, table, AX_X, ALU.add))

            def step_tiles(sums):
                link(dve.tensor_tensor(table, table, sums, ALU.mult))
                link(dve.tensor_reduce(step_t, table, AX_X, ALU.max))
                link(dve.tensor_tensor(step_t, no, step_t, ALU.subtract))

            def step_addresses():
                link(dve.tensor_scalar(step_x, step_e, float(REGION), None, ALU.mult))
                link(dve.scalar_tensor_tensor(out=step_x, in0=step_t, scalar=float(P), in1=step_x, op0=ALU.mult,
                                              op1=ALU.add))
                link(dve.tensor_scalar(step_x, step_x, float(ROW_MAX), None, ALU.min))
                dve.tensor_copy(step_row[:], step_x)
                link(dve.tensor_scalar(step_e, step_e, float(E - 1), None, ALU.min))
                link(dve.tensor_scalar(step_t, step_e, float(WE), None, ALU.mult))
                dve.tensor_copy(step_at[:], step_t).then_inc(tables_ready, 1)

            counts = bank[5][:, 0:E]
            no = step_no[:]
            paddings()
            stage_rows(B - 1, (B - 1) % 2, 2)
            sums = tile_sums()
            stage_rows(B - 1, (B - 1) % 2, 3)
            step_experts(sums)
            stage_rows(B - 1, (B - 1) % 2, 4)
            step_tiles(sums)
            stage_rows(B - 1, (B - 1) % 2, 5)
            step_addresses()
            stage_rows(B - 1, (B - 1) % 2, 6)
            stage_rows(B - 1, (B - 1) % 2, 7)

            def step(m, c):
                s = m * RING + c
                if live(s - 2):
                    r = c % 2
                    dve.wait_ge(high_ready, s - 1)
                    dve.tensor_tensor(act_hl[:, r, D:2 * D], act_t[:, r, :], act_hl[:, r, 0:D],
                                      ALU.subtract).then_inc(low_ready, 1)
                if live(s - 1):
                    r = (c - 1) % 2
                    h = bank[2 + r]
                    dve.wait_ge(h_done, s)
                    dve.tensor_scalar(a_t[:, r, :], h[:, 0:D], 1.0 / H_SCALE, LIMIT, ALU.mult,
                                      ALU.min).then_inc(a_ready, 1)
                    dve.tensor_scalar(b_t[:, r, :], h[:, D:2 * D], LIMIT * H_SCALE, -LIMIT * H_SCALE, ALU.min,
                                      ALU.max).then_inc(h_used, 1)
                if live(s - 3):
                    r = (c - 3) % 2
                    dve.wait_ge(act_turned, s - 2)
                    wait(dve, y_done, s - 4)
                    dve.tensor_copy(actT[:, r, :], bank[4 + r][:, :].bitcast(F16)[:, 0:4 * P]).then_inc(act_copied, 1)
                if live(s - 1):
                    r = (c - 1) % 2
                    dve.wait_ge(h_used, s)
                    dve.scalar_tensor_tensor(out=m_t[:, r, :], in0=b_t[:, r, :], scalar=H_SCALE, in1=a_t[:, r, :],
                                             op0=ALU.add, op1=ALU.mult).then_inc(m_ready, 1)
                    dve.wait_ge(sig_ready, s)
                    dve.wait_ge(m_ready, s)
                    dve.scalar_tensor_tensor(out=act_t[:, r, :], in0=m_t[:, r, :], scalar=A_SCALE / H_SCALE,
                                             in1=sig_t[:, r, :], op0=ALU.mult, op1=ALU.mult).then_inc(act_ready, 1)

            for c in range(RING):
                step(0, c)
            with dve.Fori(1, ROUNDS) as m:
                for c in range(RING):
                    step(m, c)
            for c in range(3):
                step(ROUNDS, c)

            def end(b):
                wait(dve, scaled, TB * b)
                for j in range(TB):
                    dve.wait_ge(pairs_added, TB * b + j + 1)
                    dve.tensor_tensor(summed_t[:, j, :], part[:, j, 0:D], part[:, j, D:2 * D],
                                      ALU.add).then_inc(ffn_summed, 1)
                    dve.wait_ge(ffn_in_ready, TB * b + j + 1)
                    dve.wait_ge(ffn_summed, 2 * (TB * b + j) + 1)
                    dve.tensor_tensor(summed_t[:, j, :], summed_t[:, j, :], ffn[:, j, :],
                                      ALU.add).then_inc(ffn_summed, 1)
                    dve.wait_ge(ffn_summed, 2 * (TB * b + j) + 2)
                    last = dve.bn_stats(stats[:, j, :], summed_t[:, j, :])
                link(last, apart)
                for j in range(TB):
                    last = dve.bn_aggr(mv[:, j, :], stats[:, j, :])
                link(last)
                power(mv[:, :, 1], 1.0, 4 * B + b + 2)
                for j in range(TB):
                    dve.tensor_scalar(summed_t[:, j, :], summed_t[:, j, :], mv[:, j, 0:1], rstd[:, j:j + 1],
                                      ALU.subtract, ALU.mult).then_inc(shifted, 1)
                wait(dve, out_stored, 16 * b)
                for j in range(TB):
                    dve.wait_ge(shifted, TB * b + j + 1)
                    dve.tensor_tensor(fin[:, j, :], summed_t[:, j, :], tile_x(b, j), ALU.add).then_inc(scaled, 1)

            for c in range(RING):
                dve.wait_ge(result_sent[c], 16 * ROUNDS)
            start = steps.passed()
            end(0)
            per_batch = steps.n
            with dve.Fori(1, B) as b:
                steps.base, steps.n = b * per_batch + start, 0
                end(b)


_INS = ["L0_attn_x", "L0_attn_Wq", "L0_attn_Wk", "L0_attn_Wv", "L0_attn_Wo", "L0_ffn_norm_w", "L0_ffn_gate_w",
        "L0_ffn_gate_b", "L0_ffn_w1", "L0_ffn_b1", "L0_ffn_w2", "L0_ffn_b2"]


def kernel(**inputs):
    import numpy as np
    import concourse.bacc as bacc
    from concourse.bass_utils import run_bass_kernel_spmd

    nc = bacc.Bacc("TRN2", target_bir_lowering=False, num_devices=1)
    arrays, args = {}, []
    for name in _INS:
        a = np.ascontiguousarray(inputs[name])
        arrays[f"in_{name}"] = a
        args.append(nc.dram_tensor(f"in_{name}", a.shape, mybir.dt.from_np(a.dtype), kind="ExternalInput").ap())
    out = nc.dram_tensor("out", arrays["in_L0_attn_x"].shape, F32, kind="ExternalOutput").ap()
    moe_block(nc, *args, out)
    r = run_bass_kernel_spmd(nc, [arrays], core_ids=[0])
    return r.results[0]["out"]
```

```python
from contextlib import ExitStack

import concourse.bass as bass
from concourse import mybir

ALU = mybir.AluOpType
ACT = mybir.ActivationFunctionType
AX_X = mybir.AxisListType.X
F32 = mybir.dt.float32
F16 = mybir.dt.float16
BF16 = mybir.dt.bfloat16
I32 = mybir.dt.int32
U32 = mybir.dt.uint32

P = 128
EPS = 1e-5
LIMIT = 7.0
ALPHA = 1.702
TOP = 4
HEADS = 32
U_SCALE = 64.0
W_SCALE = 256.0
A_SCALE = 64.0
H_SCALE = U_SCALE * W_SCALE
Y_SCALE = A_SCALE * W_SCALE


def wait(engine, semaphore, value):
    if not isinstance(value, int) or value > 0:
        engine.wait_ge(semaphore, value)


class Steps:

    def __init__(self, engine, semaphore):
        self.engine, self.semaphore, self.base, self.n = engine, semaphore, 0, 0

    def link(self, instruction, apart=None):
        self.n += 1
        instruction.then_inc(self.semaphore, 1)
        self.engine.wait_ge(self.semaphore, self.base + self.n)
        if apart:
            apart(self.engine)

    def passed(self):
        self.base, self.n = self.base + self.n, 0
        return self.base


def moe_block(nc, x, wq, wk, wv, wo, norm_w, gate_w, gate_b, w1, b1, w2, b2, out):
    B, S, D = x.shape
    E, O, _ = w1.shape
    C = D // P
    assert C == 2 and O == 2 * D and w2.shape == (E, D, D) and S % P == 0
    TB = S // P
    N = B * S
    REGION = N + P
    RING = 8
    STEPS = -(-(N * TOP // P + E - 1) // RING) * RING
    ROUNDS = STEPS // RING
    FIRST, TURN, SECOND = 1, 3, 4
    SCALE = SECOND + 1
    ROW = D + 2
    TOKEN, GATE = D, D + 1
    W1PART = C * O
    W2PART = C * D
    PICK = 2 * (W1PART + W2PART)
    WE = PICK + P
    SCORE_SCALE = float(D // HEADS) ** -0.5
    ROW_MAX = E * REGION
    POWERS = 3 * B + 1
    HALF = [range(TB // 2), range(TB // 2, TB)]
    FILLS = 3 * (E // B)
    assert FILLS == 12 and TB == 8 and B % 2 == 0

    x_dram = x.rearrange("b (p j) d -> (b p) (j d)", p=P)
    out_dram = out.rearrange("b (p j) d -> (b p) (j d)", p=P)
    rows = nc.dram_tensor("expert_rows", [(E + 1) * REGION, ROW], F32).ap()
    sums = [nc.dram_tensor(f"result_sums{i}", [N, D], F32).ap() for i in range(2)]
    sums_dram = [of.rearrange("(q j) d -> q (j d)", j=TB) for of in sums]

    with ExitStack() as ctx:
        def sb(name, shape, dt=F32):
            return ctx.enter_context(nc.sbuf_tensor(name, shape, dt))

        def sem(name):
            return ctx.enter_context(nc.semaphore(name))

        X = sb("X", [P, B * TB * D])
        W = sb("W", [P, E * WE], F16)
        bias_rows = sb("bias_rows", [96, O], BF16)
        ident = sb("ident", [P, P])
        ident16 = sb("ident16", [P, P], F16)
        ident_bf = sb("ident_bf", [P, P], BF16)
        below = sb("below", [P, P], BF16)
        ones = sb("ones", [P, P], BF16)
        wqs = sb("wqs", [P, C, D])
        wks = sb("wks", [P, C, D])
        wvT = sb("wvT", [P, C, D])
        wos = sb("wos", [P, C, D])
        gateT = sb("gateT", [P, C, E])
        gate_b_all = sb("gate_b_all", [P, E])
        norm = sb("norm", [P, C])
        norm_scaled = sb("norm_scaled", [P, C])
        pow_half = sb("pow_half", [P, TB])
        expert_no = sb("expert_no", [P, E])
        token = sb("token", [P, B * TB], I32)
        zero_rows = sb("zero_rows", [P, ROW])
        step_at = sb("step_at", [1, STEPS], I32)
        step_row = sb("step_row", [1, STEPS], I32)
        pad_row = sb("pad_row", [1, E + 1], I32)
        ffn_rstd = sb("ffn_rstd", [P, B * TB])
        ffn_bias = sb("ffn_bias", [P, B * TB])
        stats = sb("stats", [P, TB, 6])
        mv = sb("mv", [P, TB, 2])
        var_eps = sb("var_eps", [P, 2, TB])
        rstd_both = sb("rstd_both", [P, 2, TB])
        rstd, rstd_next = rstd_both[:, 0, :], rstd_both[:, 1, :]
        row_max = sb("row_max", [P, C])
        row_neg = sb("row_neg", [P, C])
        row_sum = sb("row_sum", [P, C])
        row_inv = sb("row_inv", [P, C])
        wo_mean = sb("wo_mean", [P, C])
        logits = sb("logits", [P, TB, E])
        top_v = sb("top_v", [P, TB, 8])
        top_i = sb("top_i", [P, TB, 8], U32)
        top_e = sb("top_e", [P, B * TB * TOP])
        gate_e = sb("gate_e", [P, TB, TOP])
        gate_sum = sb("gate_sum", [P, TB])
        gate_inv = sb("gate_inv", [P, TB])
        gates = sb("gates", [P, B * TB * TOP])
        onehot = sb("onehot", [P, TB * TOP, E])
        chosen = sb("chosen", [P, TB, E], BF16)
        batch_count = sb("batch_count", [P, E])
        count = sb("count", [P, E], BF16)
        rank = sb("rank", [P, TB * TOP])
        row_f = sb("row_f", [P, TB * TOP])
        row_i = sb("row_i", [P, 2, TB * TOP], U32)
        x_mean = sb("x_mean", [P, 2, TB])
        x_mean_neg = sb("x_mean_neg", [P, (B + 1) * TB])
        squares = sb("squares", [P, 2, TB])
        end_bias = sb("end_bias", [P, TB])
        square_out = sb("square_out", [P, 2, D], BF16)
        stage = sb("stage", [P, 2, TOP, ROW])
        raw1 = sb("raw1", [P, 2, C, O])
        raw2 = sb("raw2", [P, 2, C, D])
        cum = sb("cum", [P, 2, E])
        tile_f = sb("tile_f", [P, E])
        tile_i = sb("tile_i", [P, E], I32)
        step_no = sb("step_no", [1, STEPS])
        pad_f = sb("pad_f", [1, E + 1])
        pad_base = sb("pad_base", [1, E + 1])
        AREA = 4 * TB * D + 2 * D
        area = sb("area", [P, AREA])

        def views(sizes, of=area, dt=F32):
            at, made = 0, []
            for n in sizes:
                made.append(of[:, at:at + n])
                at += n
            assert at <= of.shape[1]
            return made

        turns, xnT, gram, prod, mixer, uT = views([2 * TB * D, C * S, C * D, C * D, C * D, 2 * 512])
        xnT, gram, prod, mixer = (v.rearrange("p (c d) -> p c d", c=C) for v in (xnT, gram, prod, mixer))
        probs = gram
        uT = uT.rearrange("p (r n) -> p r n", r=2)

        def turn_of(side, j):
            return turns[:, side * TB * D + j * D:side * TB * D + (j + 1) * D]

        table = area[0:1, 2 * TB * D:2 * TB * D + STEPS * E].rearrange("p (s e) -> p s e", e=E)
        step_e, step_t, step_x = (
            area[0:1, 2 * TB * D + STEPS * (E + n):2 * TB * D + STEPS * (E + n + 1)] for n in range(3))
        tiles, utp, a_t, b_t, sig_t, m_t, act_t, act_hl, actT, y_t = views(
            [RING * ROW, 2 * D, 2 * D, 2 * D, 2 * D, 2 * D, 2 * D, 2 * D, 2 * D, 4 * D])
        tiles = tiles.rearrange("p (r n) -> p r n", r=RING)
        utp, act_hl, actT = (
            v.bitcast(F16).rearrange("p (r n) -> p r n", r=2) for v in (utp, act_hl, actT))
        a_t, b_t, sig_t, m_t, act_t = (
            v.rearrange("p (r n) -> p r n", r=2) for v in (a_t, b_t, sig_t, m_t, act_t))
        y_t = y_t.rearrange("p (r n) -> p r n", r=4)
        got, part, ffn, scaled_t, fin, gate_rows = views(
            [TB * 2 * D, TB * D, TB * D, TB * D, TB * D, N // 2], of=W[:, :].bitcast(F32))
        got = got.rearrange("p (i n) -> p i n", i=2)
        part, ffn, scaled_t, fin = (v.rearrange("p (j d) -> p j d", j=TB) for v in (part, ffn, scaled_t, fin))
        gate_rows = gate_rows.bitcast(BF16)
        gate_cols = raw2[:, 1].rearrange("p c n -> p (c n)").rearrange("p (t e) -> p t e", e=E)
        gate_parts = raw1[:].rearrange("p r c n -> p (r c n)").bitcast(BF16)
        assert 2 * E == P // 4 and gate_parts.shape[1] == N
        gate_quarters = gate_parts.rearrange("p (t q i e) -> p t q i e", q=4, i=2, e=E)
        b2_f, b2_parts = raw2[:, 0, 0, :], raw2[:, 0, 1, 0:D // 2].bitcast(BF16)
        picks = W[0:96, :].bitcast(BF16).rearrange("p (e w) -> p e w", e=E)[:, :, PICK:PICK + P]
        wv_raw = raw2[:, 0]
        gate_raw = raw1[0:E, 0, 0, 0:D]
        wo_raw = raw2[:, 1]
        bias_f = raw1[0:96, 1].rearrange("p c n -> p (c n)")[:, 0:O]
        bias_t = raw1[0:96, 0].rearrange("p c n -> p (c n)")[:, 0:O]

        bank = [ctx.enter_context(nc.psum_tensor(f"bank{i}", [P, 512], F32)) for i in range(8)]

        x_loaded = [sem(f"x_loaded{i}") for i in range(2)]
        attn_w_loaded = sem("attn_w_loaded")
        setup_loaded = sem("setup_loaded")
        bias_loaded = sem("bias_loaded")
        raw_loaded = [sem(f"raw_loaded{i}") for i in range(2)]
        rows_sent = [sem(f"rows_sent{i}") for i in range(2)]
        pads_written = sem("pads_written")
        tile_loaded = [sem(f"tile_loaded{i}") for i in range(RING)]
        result_sent = [sem(f"result_sent{i}") for i in range(RING)]
        got_loaded = [sem(f"got_loaded{i}") for i in range(TB // 2)]
        zeros_ready = sem("zeros_ready")
        sums_zeroed = sem("sums_zeroed")
        out_stored = [sem(f"out_stored{i}") for i in range(2)]
        wait_over = sem("wait_over")
        consts = sem("consts")
        pool_first = sem("pool_first")
        bias_zeroed = sem("bias_zeroed")
        setup_turned = sem("setup_turned")
        wv_turned_copied = sem("wv_turned_copied")
        setup_done = sem("setup_done")
        bias_ready = sem("bias_ready")
        dve_step = sem("dve_step")
        var_ready = sem("var_ready")
        rstd_ready = sem("rstd_ready")
        xn_ready = sem("xn_ready")
        gram_done = sem("gram_done")
        gram_copied = sem("gram_copied")
        xn_turned = sem("xn_turned")
        xnT_copied = sem("xnT_copied")
        prod_done = sem("prod_done")
        prod_copied = sem("prod_copied")
        scores_done = sem("scores_done")
        max_ready = sem("max_ready")
        exp_done = sem("exp_done")
        probs_ready = sem("probs_ready")
        mixer_done = sem("mixer_done")
        mixer_copied = sem("mixer_copied")
        att_done = sem("att_done")
        squared = sem("squared")
        x_added = sem("x_added")
        u_ready = sem("u_ready")
        hi_staged = sem("hi_staged")
        u_turned_front = sem("u_turned_front")
        uT_copied_front = sem("uT_copied_front")
        logits_done = sem("logits_done")
        gate_in_ready = sem("gate_in_ready")
        gate_exp_done = sem("gate_exp_done")
        chosen_ready = sem("chosen_ready")
        rank_done = sem("rank_done")
        staged = sem("staged")
        w_turned = sem("w_turned")
        w_high = sem("w_high")
        w_low = sem("w_low")
        counts_done = sem("counts_done")
        counted = sem("counted")
        tables_ready = sem("tables_ready")
        pad_ready = sem("pad_ready")
        u_turned = sem("u_turned")
        u_copied = sem("u_copied")
        h_done = sem("h_done")
        a_ready = sem("a_ready")
        h_used = sem("h_used")
        m_ready = sem("m_ready")
        sig_ready = sem("sig_ready")
        act_ready = sem("act_ready")
        high_ready = sem("high_ready")
        low_ready = sem("low_ready")
        act_turned = sem("act_turned")
        act_copied = sem("act_copied")
        y_done = sem("y_done")
        y_ready = sem("y_ready")
        ffn_powers = sem("ffn_powers")
        ffn_scales_ready = sem("ffn_scales_ready")
        ffn_in_ready = sem("ffn_in_ready")
        pair_added = sem("pair_added")
        b2_loaded = sem("b2_loaded")
        gate_cols_ready = sem("gate_cols_ready")
        gate_parts_zeroed = sem("gate_parts_zeroed")
        gate_parts_ready = sem("gate_parts_ready")
        b2_ready = sem("b2_ready")
        gates_turned = sem("gates_turned")
        gates_copied = sem("gates_copied")
        ffn_summed = sem("ffn_summed")
        ffn_scale_ready = sem("ffn_scale_ready")
        scaled = sem("scaled")
        finished = sem("finished")

        block = ctx.enter_context(nc.Block())

        def tile_x(b, j):
            return X[:, bass.ds(b * (TB * D) + j * D, D)]

        def halves(i):
            return [bank[i][:, 0:D], bank[i][:, D:2 * D]]

        def apart(engine):
            engine.sem_inc(wait_over, 1)

        def live(s):
            return not isinstance(s, int) or 0 <= s < STEPS

        @block.sync
        def _(sp):
            for b in range(B):
                for n in range(2):
                    wait(sp, x_loaded[n], 16 * b)
                    half = slice(n * TB // 2 * D, (n + 1) * TB // 2 * D)
                    sp.dma_start(X[:, b * TB * D:(b + 1) * TB * D][:, half],
                                 x_dram[b * P:(b + 1) * P, half]).then_inc(x_loaded[n], 16)
                if b == 0:
                    for w, to in ((wk, wks), (wq, wqs)):
                        sp.dma_start(to[:], w.rearrange("(c p) f -> p c f", p=P)).then_inc(attn_w_loaded, 16)
                    for w, to in ((wv, wv_raw), (wo, wo_raw)):
                        sp.dma_start(to, w.rearrange("(c p) f -> p c f", p=P)).then_inc(setup_loaded, 16)
                    sp.dma_start(gate_raw, gate_w).then_inc(setup_loaded, 16)
                    sp.dma_start(norm[:], norm_w.rearrange("(c p) -> p c", p=P),
                                 allow_slow_non_contiguous=True).then_inc(setup_loaded, 16)
                    sp.dma_start(gate_b_all[:], gate_b.partition_broadcast(P)).then_inc(setup_loaded, 16)
                    sp.wait_ge(bias_zeroed, 1)
                    for part_no in range(3):
                        to = bias_f[32 * part_no:32 * part_no + E, :]
                        sp.dma_start(to, b1).then_inc(bias_loaded, 16)

            sp.wait_ge(setup_done, 1)
            sp.wait_ge(bias_ready, 3)

            def load_expert(e, r):
                wait(sp, w_low, 3 * (e - 1))
                for q in range(C):
                    w1_e = w1.rearrange("e (r c) h -> (e r) (c h)", c=2)
                    sp.dma_start(raw1[:, r, q, :], w1_e[bass.ds(e * D + q * P, P), :]).then_inc(raw_loaded[r], 16)
                    w2_e = w2.rearrange("e d i -> (e d) i")
                    sp.dma_start(raw2[:, r, q, :], w2_e[bass.ds(e * D + q * P, P), :]).then_inc(raw_loaded[r], 16)

            for r in range(2):
                load_expert(r, r)
            sp.wait_ge(zeros_ready, 1)
            for of in sums:
                sp.dma_start(of.rearrange("(p n) d -> p n d", p=P),
                             zero_rows[:, 0:D].unsqueeze(1).to_broadcast([P, N // P, D])).then_inc(sums_zeroed, 16)
            with sp.Fori(1, E // 2) as k:
                for r in range(2):
                    load_expert(k * 2 + r, r)

            sp.wait_ge(pad_ready, 1)
            with sp.Fori(0, E + 1) as e:
                at = sp.value_load(pad_row[0:1, bass.ds(e, 1)], min_val=0, max_val=ROW_MAX)
                sp.dma_start(rows[bass.ds(at, P), :], zero_rows[:]).then_inc(pads_written, 16)
            sp.wait_ge(w_low, 3 * E)
            for n in range(P // E):
                sp.dma_start(b2_f[n * E:(n + 1) * E, :], b2).then_inc(b2_loaded, 16)
            sp.wait_ge(tables_ready, 1)
            sp.wait_ge(pads_written, 16 * (E + 1))
            for i in range(2):
                sp.wait_ge(rows_sent[i], 16 * TOP * B * TB // 2)

            def load_tile(m, c):
                at = sp.value_load(step_row[0:1, bass.ds(m * RING + c, 1)], min_val=0, max_val=ROW_MAX)
                wait(sp, result_sent[c], 16 * m)
                sp.dma_start(tiles[:, c, :], rows[bass.ds(at, P), :]).then_inc(tile_loaded[c], 16)

            for c in range(RING):
                load_tile(0, c)
            with sp.Fori(1, ROUNDS) as m:
                for c in range(RING):
                    load_tile(m, c)

            for c in range(RING):
                sp.wait_ge(result_sent[c], 16 * ROUNDS)

            def load_results(b, n):
                for t in range(n * TB // 4, (n + 1) * TB // 4):
                    wait(sp, pair_added, (b - 1) * TB + 2 * t + 2)
                    pair = slice(2 * t * D, 2 * (t + 1) * D)
                    for i in range(2):
                        sp.dma_start(got[:, i, pair], sums_dram[i][bass.ds(b * P, P), pair]).then_inc(got_loaded[t], 16)

            def store(b, n):
                sp.wait_ge(finished, b * TB + (n + 1) * (TB // 2))
                half = slice(n * TB // 2 * D, (n + 1) * TB // 2 * D)
                sp.dma_start(out_dram[bass.ds(b * P, P), half],
                             fin.rearrange("p j d -> p (j d)")[:, half]).then_inc(out_stored[n], 16)

            for b in range(2):
                for n in range(2):
                    load_results(b, n)
            store(0, 0)
            with sp.Fori(2, B) as b:
                for n in range(2):
                    load_results(b, n)
                    store(b - 2 + n, 1 - n)
            store(B - 2, 1)
            for n in range(2):
                store(B - 1, n)
            for n in range(2):
                sp.wait_ge(out_stored[n], 16 * B)

        @block.gpsimd
        def _(pool):
            pool.memset(raw1[:, 1], 0.0).then_inc(bias_zeroed, 1)
            pool.memset(pow_half[:], -0.5).then_inc(consts, 1)
            pool.memset(ident[:], 0.0).then_inc(pool_first, 1)
            pool.wait_ge(pool_first, 1)
            pool.affine_select(out=ident[:], in_=ident[:], compare_op=ALU.not_equal, fill=1.0, base=0,
                               pattern=[[-1, P]], channel_multiplier=1).then_inc(consts, 1)
            pool.memset(ones[:], 1.0).then_inc(pool_first, 1)
            pool.wait_ge(pool_first, 2)
            pool.affine_select(out=below[:], in_=ones[:], compare_op=ALU.is_gt, fill=0.0, base=0,
                               pattern=[[1, P]], channel_multiplier=-1).then_inc(consts, 1)
            pool.iota(expert_no[:], pattern=[[1, E]], base=0, channel_multiplier=0,
                      allow_small_or_imprecise_dtypes=True).then_inc(consts, 1)
            pool.iota(token[:].rearrange("p (b t) -> p b t", b=B), pattern=[[P * TB, B], [1, TB]],
                      base=0, channel_multiplier=TB).then_inc(consts, 1)
            pool.memset(zero_rows[:, 0:D], 0.0).then_inc(zeros_ready, 1)
            pool.memset(zero_rows[:, GATE:GATE + 1], 0.0).then_inc(consts, 1)
            pool.iota(zero_rows[:, TOKEN:TOKEN + 1].bitcast(I32), pattern=[[0, 1]], base=N,
                      channel_multiplier=0).then_inc(consts, 1)
            pool.iota(step_no[:], pattern=[[1, STEPS]], base=0, channel_multiplier=0,
                      allow_small_or_imprecise_dtypes=True).then_inc(consts, 1)
            pool.iota(pad_base[:], pattern=[[REGION, E + 1]], base=0, channel_multiplier=0,
                      allow_small_or_imprecise_dtypes=True).then_inc(consts, 1)

            def power(n, which=0, tiles=slice(0, TB)):
                pool.wait_ge(var_ready, n)
                pool.tensor_tensor(rstd_both[:, which, tiles], var_eps[:, which, tiles], pow_half[:, tiles],
                                   ALU.pow).then_inc(rstd_ready, 1)

            def ffn_scales(b):
                at = slice(b * TB, (b + 1) * TB)
                pool.tensor_tensor(ffn_rstd[:, at], ffn_rstd[:, at], pow_half[:], ALU.pow).then_inc(ffn_powers, 1)
                pool.wait_ge(ffn_powers, b + 1)
                pool.tensor_tensor(ffn_bias[:, at], x_mean_neg[:, at], ffn_rstd[:, at],
                                   ALU.mult).then_inc(ffn_scales_ready, 1)

            def scatter(b, side, j):
                pool.wait_ge(staged, TB * b + j + 1)
                apart(pool)
                for k in range(TOP):
                    pool.indirect_dma_start(
                        rows, bass.IndirectOffsetOnAxis(ap=row_i[:, side, j * TOP + k:j * TOP + k + 1], axis=0),
                        stage[:, j % 2, k, :], None).then_inc(rows_sent[j % 2], 16)

            def front(i, side, next_batch=True, last_batch=True):
                if last_batch:
                    scatter(i - 1, 1 - side, 2)
                power(3 * i + 3)
                if last_batch:
                    scatter(i - 1, 1 - side, 3)
                power(3 * i + 4)
                if last_batch:
                    for j in range(4, 7):
                        scatter(i - 1, 1 - side, j)
                if next_batch:
                    power(3 * i + 5, 1)
                if last_batch:
                    scatter(i - 1, 1 - side, 7)
                for j in range(2):
                    scatter(i, side, j)

            power(1, 1)
            pool.memset(picks, 0.0).then_inc(pool_first, 1)
            for part_no in range(3):
                pool.wait_ge(pool_first, 3 + part_no)
                pool.affine_select(out=picks, in_=picks, compare_op=ALU.not_equal, fill=1.0, base=-32 * part_no,
                                   pattern=[[-1, E], [0, P]], channel_multiplier=1).then_inc(pool_first, 1)
            power(2, 1)
            front(0, 0, last_batch=False)
            with pool.Fori(0, (B - 2) // 2) as k:
                front(2 * k + 1, 1)
                front(2 * k + 2, 0)
            front(B - 1, (B - 1) % 2, next_batch=False)
            for j in range(2, TB):
                scatter(B - 1, (B - 1) % 2, j)
            for b in range(B):
                ffn_scales(b)
            pool.wait_ge(w_low, 3 * E)
            pool.memset(gate_quarters[:, :, 3, 1, :], 0.0).then_inc(gate_parts_zeroed, 1)

            def send(m, c):
                pool.wait_ge(y_ready, m * RING + c + 1)
                q, slot = divmod(c - 2, RING)
                wait(pool, result_sent[slot], 16 * (m + q + 1))
                apart(pool)
                pool.indirect_dma_start(
                    sums[c % 2], bass.IndirectOffsetOnAxis(ap=tiles[:, c, TOKEN:TOKEN + 1].bitcast(U32), axis=0),
                    y_t[:, c % 4, :], None, bounds_check=last_token, oob_is_err=False,
                    compute_op=ALU.add).then_inc(result_sent[c], 16)

            last_token = pool.to_reg(N - 1)
            pool.wait_ge(sums_zeroed, 32)
            for c in range(RING):
                send(0, c)
            with pool.Fori(1, ROUNDS) as m:
                for c in range(RING):
                    send(m, c)

            def add(b, n):
                for j in HALF[n]:
                    if j % 2 == 0:
                        pool.wait_ge(got_loaded[j // 2], 32 * (b + 1))
                    wait(pool, ffn_summed, (b - 1) * TB + j + 1)
                    pool.tensor_tensor(part[:, j, :], got[:, 0, j * D:(j + 1) * D], got[:, 1, j * D:(j + 1) * D],
                                       ALU.add).then_inc(pair_added, 1)

            def half_power(b, n):
                power(POWERS + 2 * b + n + 1, tiles=slice(HALF[n][0], HALF[n][-1] + 1))

            for n in range(2):
                add(0, n)
            half_power(0, 0)
            with pool.Fori(1, B) as b:
                add(b, 0)
                half_power(b - 1, 1)
                add(b, 1)
                half_power(b, 0)
            half_power(B - 1, 1)

        @block.scalar
        def _(act):
            def copy(to, of):
                return act.activation(to, of, ACT.Copy)

            act.wait_ge(setup_turned, 1)
            copy(wvT[:].rearrange("p c d -> p (c d)"), bank[6][:, :]).then_inc(wv_turned_copied, 1)

            def gram_out(b):
                act.wait_ge(gram_done, b + 1)
                copy(gram.rearrange("p c d -> p (c d)"), bank[4][:, :]).then_inc(gram_copied, 1)

            def turned_out(b, t):
                act.wait_ge(xn_turned, TB // 2 * b + t + 1)
                wait(act, att_done, TB // 2 * b)
                copy(xnT[:, :, t * 2 * P:(t + 1) * 2 * P],
                     bank[6 + t % 2][:, :].rearrange("p (c n) -> p c n", c=C)).then_inc(xnT_copied, 1)

            def prod_out(n):
                act.wait_ge(prod_done, n)
                copy(prod.rearrange("p c d -> p (c d)"), bank[5][:, :]).then_inc(prod_copied, 1)

            def exp_scores(b):
                act.wait_ge(max_ready, b + 1)
                for c in range(C):
                    last = act.activation(probs[:, c, :], halves(4)[c], ACT.Exp, bias=row_neg[:, c:c + 1],
                                          scale=SCORE_SCALE, accum_out=row_sum[:, c:c + 1])
                last.then_inc(exp_done, 1)

            def mixer_out(b):
                act.wait_ge(mixer_done, b + 1)
                wait(act, att_done, TB // 2 * b)
                copy(mixer.rearrange("p c d -> p (c d)"), bank[4][:, :]).then_inc(mixer_copied, 1)

            def u_out(b, t):
                act.wait_ge(u_turned_front, TB // 2 * b + t + 1)
                wait(act, logits_done, TB // 2 * b + t - 1)
                copy(uT[:, t % 2, :], bank[2 + t % 2][:, :]).then_inc(uT_copied_front, 1)

            def high_rows(b, side, j):
                act.wait_ge(u_ready, TB * b + j + 1)
                wait(act, rows_sent[j % 2], 16 * TOP * (TB // 2 * b + j // 2))
                copy(stage[:, j % 2, 0, 0:P].bitcast(F16), turn_of(side, j)).then_inc(hi_staged, 1)

            def high_weights(i, n):
                part_no, at = n % 3, i * (4 * WE) + n // 3 * WE
                act.wait_ge(w_turned, FILLS * i + n + 1)
                if part_no < C:
                    to, scale = W[:, bass.ds(at + part_no * O, O)], norm_scaled[:, part_no:part_no + 1]
                else:
                    to, scale = W[:, bass.ds(at + 2 * W1PART, W2PART)], W_SCALE
                act.activation(to, bank[6 + n % 2][:, :], ACT.Copy, scale=scale).then_inc(w_high, 1)

            def square(b, side, n):
                which, j = divmod(n, TB)
                if which == 0:
                    if j % 2 == 0:
                        act.wait_ge(att_done, TB // 2 * b + j // 2 + 1)
                    of, less = halves(j // 2)[j % 2], 0.0
                else:
                    act.wait_ge(x_added, TB * b + j + 1)
                    of, less = tile_x(b, j), x_mean_neg[:, bass.ds(b * TB + j, 1)]
                wait(act, squared, 2 * TB * b + n - 1)
                act.activation(square_out[:, n % 2, :], of, ACT.Square, bias=less,
                               accum_out=squares[:, which, j:j + 1]).then_inc(squared, 1)

            def front(i, side, next_batch=True, last_batch=True):
                def staging(j):
                    if last_batch:
                        high_rows(i - 1, 1 - side, j)

                high_weights(i, 0)
                high_weights(i, 1)
                staging(2)
                for j in range(TB):
                    square(i, side, j)
                staging(3)
                high_weights(i, 2)
                high_weights(i, 3)
                for j in range(TB):
                    square(i, side, TB + j)
                staging(4)
                if next_batch:
                    gram_out(i + 1)
                    for t in range(TB // 2):
                        turned_out(i + 1, t)
                    prod_out(2 * i + 3)
                staging(5)
                u_out(i, 0)
                u_out(i, 1)
                if next_batch:
                    exp_scores(i + 1)
                u_out(i, 2)
                u_out(i, 3)
                staging(6)
                high_weights(i, 4)
                high_weights(i, 5)
                staging(7)
                if next_batch:
                    prod_out(2 * i + 4)
                act.wait_ge(gate_in_ready, i + 1)
                act.activation(gate_e[:], gate_e[:], ACT.Exp).then_inc(gate_exp_done, 1)
                if next_batch:
                    mixer_out(i + 1)
                high_weights(i, 6)
                high_weights(i, 7)
                high_rows(i, side, 0)
                high_weights(i, 8)
                high_rows(i, side, 1)
                for n in range(9, FILLS):
                    high_weights(i, n)

            gram_out(0)
            for t in range(TB // 2):
                turned_out(0, t)
            prod_out(1)
            exp_scores(0)
            prod_out(2)
            mixer_out(0)
            front(0, 0, last_batch=False)
            with act.Fori(0, (B - 2) // 2) as k:
                front(2 * k + 1, 1)
                front(2 * k + 2, 0)
            front(B - 1, (B - 1) % 2, next_batch=False)
            for j in range(2, TB):
                high_rows(B - 1, (B - 1) % 2, j)

            def high(s, c):
                act.wait_ge(act_ready, s + 1)
                wait(act, act_turned, s - 1)
                copy(act_hl[:, c % 2, 0:D], act_t[:, c % 2, :]).then_inc(high_ready, 1)

            def scale_result(m, s, c):
                act.wait_ge(y_done, s + 1)
                q, slot = divmod(c - 4, RING)
                wait(act, result_sent[slot], 16 * (m + q + 1))
                act.activation(y_t[:, c % 4, :], bank[6 + c % 2][:, 0:D], ACT.Copy,
                               scale=tiles[:, c % RING, GATE:GATE + 1]).then_inc(y_ready, 1)

            def sigmoid(s, c):
                act.wait_ge(a_ready, s + 1)
                act.activation(sig_t[:, c % 2, :], a_t[:, c % 2, :], ACT.Sigmoid, scale=ALPHA).then_inc(sig_ready, 1)

            def rows_out(s, c):
                act.wait_ge(u_turned, s + 1)
                wait(act, h_done, s - 1)
                act.copy(utp[:, c % 2, :], bank[c % 2][:, :].bitcast(F16)[:, 0:4 * P]).then_inc(u_copied, 1)

            def step(m, c):
                s = m * RING + c
                if live(s - TURN):
                    high(s - TURN, c - TURN)
                if live(s - SCALE):
                    scale_result(m, s - SCALE, c - SCALE)
                if live(s):
                    rows_out(s, c)
                if live(s - FIRST):
                    sigmoid(s - FIRST, c - FIRST)

            act.activation(square_out[0:1, 0, 0:1], square_out[0:1, 1, 0:1], ACT.Sigmoid)
            for c in range(RING):
                step(0, c)
            with act.Fori(1, ROUNDS) as m:
                for c in range(RING):
                    step(m, c)
            for c in range(SCALE):
                step(ROUNDS, c)


            def ffn_in(b, n):
                for j in HALF[n]:
                    wait(act, ffn_summed, (b - 1) * TB + j + 1)
                    act.activation(ffn[:, j, :], tile_x(b, j), ACT.Identity,
                                   scale=ffn_rstd[:, bass.ds(b * TB + j, 1)],
                                   bias=ffn_bias[:, bass.ds(b * TB + j, 1)]).then_inc(ffn_in_ready, 1)

            def scale(b, n):
                act.wait_ge(ffn_scale_ready, 2 * b + n + 1)
                wait(act, finished, (b - 1) * TB + HALF[n][-1] + 1)
                for j in HALF[n]:
                    act.activation(scaled_t[:, j, :], bank[j][:, 0:D], ACT.Identity, scale=rstd[:, j:j + 1],
                                   bias=end_bias[:, j:j + 1]).then_inc(scaled, 1)

            def gates_out(b):
                act.wait_ge(gates_turned, b + 1)
                copy(gate_rows[:, b * TB * P:(b + 1) * TB * P], bank[b][:, :].bitcast(BF16)).then_inc(gates_copied, 1)

            act.wait_ge(ffn_scales_ready, B)
            for n in range(2):
                ffn_in(0, n)
            for b in range(B):
                gates_out(b)
            for n in range(2):
                ffn_in(1, n)
                scale(0, n)
            with act.Fori(2, B) as b:
                for n in range(2):
                    ffn_in(b, n)
                    scale(b - 1, n)
            for n in range(2):
                scale(B - 1, n)

        @block.tensor
        def _(pe):
            pe.wait_ge(consts, 2)
            pe.wait_ge(setup_loaded, 16 * 5)
            for f in range(C):
                for h in range(C):
                    last = pe.transpose(bank[6][:, f * D + h * P:f * D + (h + 1) * P],
                                        wv_raw[:, h, f * P:(f + 1) * P], ident[:, :])
            last.then_inc(setup_turned, 1)
            for h in range(C):
                last = pe.transpose(bank[7][:, h * E:(h + 1) * E], gate_raw[:, h * P:(h + 1) * P],
                                    ident[0:E, 0:E])
            last.then_inc(setup_turned, 1)
            pe.wait_ge(wv_turned_copied, 1)
            pe.wait_ge(setup_done, 1)
            pe.wait_ge(attn_w_loaded, 32)

            def square(to, left, right):
                for m in range(C):
                    for c in range(C):
                        last = pe.matmul(halves(to)[m], left[:, c, m * P:(m + 1) * P], right[:, c, :],
                                         start=(c == 0), stop=(c == C - 1))
                return last

            def gram_of(b, side):
                pe.wait_ge(xn_ready, TB * (b + 1))
                for h in range(C):
                    for j in range(TB):
                        last = pe.matmul(halves(4)[h], turn_of(side, j)[:, h * P:(h + 1) * P], turn_of(side, j),
                                         start=(j == 0), stop=(j == TB - 1))
                last.then_inc(gram_done, 1)
                for t in range(TB // 2):
                    if t < 2:
                        wait(pe, w_low, FILLS * (b - 1) + 3 + t)
                    else:
                        wait(pe, xnT_copied, TB // 2 * b + t - 1)
                    for c in range(C):
                        for j in range(2):
                            last = pe.transpose(bank[6 + t % 2][:, (2 * c + j) * P:(2 * c + j + 1) * P],
                                                turn_of(side, 2 * t + j)[:, c * P:(c + 1) * P], ident[:, :])
                    last.then_inc(xn_turned, 1)

            def scores_of(b):
                pe.wait_ge(gram_copied, b + 1)
                square(5, gram, wks).then_inc(prod_done, 1)
                pe.wait_ge(prod_copied, 2 * b + 1)
                square(4, wqs, prod).then_inc(scores_done, 1)

            def mixer_of(b):
                pe.wait_ge(probs_ready, b + 1)
                square(5, probs, wos).then_inc(prod_done, 1)
                pe.wait_ge(prod_copied, 2 * b + 2)
                square(4, wvT, prod).then_inc(mixer_done, 1)

            def attend(b):
                pe.wait_ge(mixer_copied, b + 1)
                pe.wait_ge(xnT_copied, TB // 2 * (b + 1))
                wait(pe, counted, b)
                for j in range(TB):
                    for c in range(C):
                        last = pe.matmul(halves(j // 2)[j % 2], xnT[:, c, j * P:(j + 1) * P], mixer[:, c, :],
                                         start=(c == 0), stop=(c == C - 1))
                    if j % 2:
                        last.then_inc(att_done, 1)

            def logits_of(b, side):
                def turn(t):
                    pe.wait_ge(u_ready, TB * b + 2 * t + 2)
                    wait(pe, uT_copied_front, TB // 2 * b + t - 1)
                    for j in range(2):
                        for c in range(C):
                            last = pe.transpose(bank[2 + t % 2][:, (2 * j + c) * P:(2 * j + c + 1) * P],
                                                turn_of(side, 2 * t + j)[:, c * P:(c + 1) * P], ident[:, :])
                    last.then_inc(u_turned_front, 1)

                def route(t):
                    pe.wait_ge(uT_copied_front, TB // 2 * b + t + 1)
                    for j in range(2):
                        for c in range(C):
                            last = pe.matmul(bank[0][:, (2 * t + j) * E:(2 * t + j + 1) * E],
                                             uT[:, t % 2, (2 * j + c) * P:(2 * j + c + 1) * P], gateT[:, c, :],
                                             start=(c == 0), stop=(c == C - 1))
                    last.then_inc(logits_done, 1)

                turn(0)
                for t in range(1, TB // 2):
                    turn(t)
                    route(t - 1)
                route(TB // 2 - 1)

            def ranks_of(b):
                pe.wait_ge(chosen_ready, b + 1)
                ranks = bank[1][:, 0:TB * E].rearrange("p (j e) -> p j e", e=E)
                pe.matmul(ranks, below[:, :], chosen[:, :, :], start=True, stop=False)
                for j in range(TB - 1):
                    pe.matmul(ranks[:, j + 1:TB, :], ones[:, :],
                              chosen[:, j:j + 1, :].to_broadcast([P, TB - 1 - j, E]), start=False, stop=False,
                              skip_group_check=True)
                pe.matmul(ranks, ones[:, :], count[:, :].unsqueeze(1).to_broadcast([P, TB, E]),
                          start=False, stop=True).then_inc(rank_done, 1)

            def turn_weights(i, n):
                part_no, r = n % 3, n // 3 % 2
                if part_no == 0:
                    pe.wait_ge(raw_loaded[r], i * 128 + n // 6 * 64 + 64)
                wait(pe, w_low, FILLS * i + n - 1)
                if n in (0, 4):
                    pe.wait_ge(xnT_copied, TB // 2 * (i + 1 if n == 0 or isinstance(i, int) and i == B - 1 else i + 2))
                to = bank[6 + n % 2]
                for c in range(2):
                    for q in range(C):
                        if part_no < C:
                            of = raw1[:, r, q, c * D + part_no * P:c * D + (part_no + 1) * P]
                        else:
                            of = raw2[:, r, q, c * P:(c + 1) * P]
                        last = pe.transpose(to[:, c * D + q * P:c * D + (q + 1) * P], of, ident[:, :])
                last.then_inc(w_turned, 1)

            def front(i, side, next_batch=True):
                turn_weights(i, 0)
                turn_weights(i, 1)
                attend(i)
                turn_weights(i, 2)
                turn_weights(i, 3)
                if next_batch:
                    gram_of(i + 1, side)
                    scores_of(i + 1)
                logits_of(i, side)
                turn_weights(i, 4)
                turn_weights(i, 5)
                if next_batch:
                    mixer_of(i + 1)
                ranks_of(i)
                for n in range(6, FILLS):
                    turn_weights(i, n)

            gram_of(0, 1)
            scores_of(0)
            mixer_of(0)
            front(0, 0)
            with pe.Fori(0, (B - 2) // 2) as k:
                front(2 * k + 1, 1)
                front(2 * k + 2, 0)
            front(B - 1, (B - 1) % 2, next_batch=False)

            pe.wait_ge(counted, B)
            pe.matmul(bank[5][:, 0:E], ones[:, :], count[:, :], start=True, stop=True).then_inc(counts_done, 1)

            pe.wait_ge(tables_ready, 1)
            pe.wait_ge(w_low, 3 * E)
            pe.wait_ge(bias_ready, 3)

            def turn_rows(s, c):
                pe.wait_ge(tile_loaded[c % RING], 16 * (s // RING + 1) if isinstance(s, int) else (s - c) * 2 + 16)
                wait(pe, u_copied, s - 1)
                of = tiles[:, c % RING, 0:D].bitcast(F16)
                to = bank[c % 2][:, :].bitcast(F16)
                for k in range(4):
                    last = pe.transpose(to[:, k * P:(k + 1) * P], of[:, k * P:(k + 1) * P], ident16[:, :])
                last.then_inc(u_turned, 1)

            def first(s, c, at):
                pe.wait_ge(u_copied, s + 1)
                wait(pe, h_used, s - 1)
                to = bank[2 + c % 2][:, :]
                pe.matmul(to, W[0:96, bass.ds(at + PICK, P)].bitcast(BF16), bias_rows[:, 0:O], start=True, stop=False)
                n = 0
                for h in range(C):
                    for u_part, w_part in ((0, 0), (1, 0), (0, 1)):
                        n += 1
                        last = pe.matmul(to, utp[:, c % 2, (2 * u_part + h) * P:(2 * u_part + h + 1) * P],
                                         W[:, bass.ds(at + (w_part * W1PART + h * O), O)],
                                         start=False, stop=(n == 3 * C))
                last.then_inc(h_done, 1)

            def turn_act(s, c):
                pe.wait_ge(low_ready, s + 1)
                wait(pe, act_copied, s - 1)
                to = bank[4 + c % 2][:, :].bitcast(F16)
                for k in range(4):
                    last = pe.transpose(to[:, k * P:(k + 1) * P], act_hl[:, c % 2, k * P:(k + 1) * P], ident16[:, :])
                last.then_inc(act_turned, 1)

            def second(s, c, at):
                pe.wait_ge(act_copied, s + 1)
                wait(pe, y_ready, s - 1)
                to = bank[6 + c % 2][:, 0:D]
                n = 0
                for h in range(C):
                    for a_part, w_part in ((0, 0), (1, 0), (0, 1)):
                        n += 1
                        last = pe.matmul(to, actT[:, c % 2, (2 * a_part + h) * P:(2 * a_part + h + 1) * P],
                                         W[:, bass.ds(at + (2 * W1PART + w_part * W2PART + h * D), D)],
                                         start=(n == 1), stop=(n == 3 * C))
                last.then_inc(y_done, 1)

            starts = [pe.alloc_register(f"weights_at{c}") for c in range(RING)]

            def start_of(c):
                return pe.snap(starts[c % RING], min_val=0, max_val=(E - 1) * WE)

            def step(m, c):
                s = m * RING + c
                if live(s - FIRST):
                    first(s - FIRST, c - FIRST, start_of(c - FIRST))
                if live(s):
                    pe.load(starts[c], step_at[0:1, bass.ds(s, 1)])
                if live(s):
                    turn_rows(s, c)
                if live(s - TURN):
                    turn_act(s - TURN, c - TURN)
                if live(s - SECOND):
                    second(s - SECOND, c - SECOND, start_of(c - SECOND))

            for c in range(RING):
                step(0, c)
            with pe.Fori(1, ROUNDS) as m:
                for c in range(RING):
                    step(m, c)
            for c in range(SECOND):
                step(ROUNDS, c)

            for read in (y_ready, act_copied, h_used, u_copied):
                pe.wait_ge(read, STEPS)
            for b in range(B):
                pe.wait_ge(gate_parts_ready, b + 1)
                for j in range(TB):
                    tile = b * TB + j
                    last = pe.transpose(bank[b][:, :].bitcast(BF16)[:, j * P:(j + 1) * P],
                                        gate_parts[:, tile * P:(tile + 1) * P], ident_bf[:, :])
                last.then_inc(gates_turned, 1)
            pe.wait_ge(b2_ready, 1)
            pe.wait_ge(gates_copied, B)

            def sum_ffn(b):
                for j in range(TB):
                    wait(pe, scaled, (b - 1) * TB + j + 1)
                    to, tile = bank[j][:, 0:D], b * TB + j
                    pe.matmul(to, gate_rows[:, bass.ds(tile * P, P)], b2_parts, start=True, stop=False)
                    pe.wait_ge(ffn_in_ready, tile + 1)
                    pe.matmul(to, ident[:, :], ffn[:, j, :], start=False, stop=False)
                    pe.wait_ge(pair_added, tile + 1)
                    pe.matmul(to, ident[:, :], part[:, j, :], start=False, stop=True).then_inc(ffn_summed, 1)

            sum_ffn(0)
            with pe.Fori(1, B) as b:
                sum_ffn(b)

        @block.vector
        def _(dve):
            steps = Steps(dve, dve_step)
            link = steps.link

            dve.wait_ge(consts, 4)
            dve.tensor_copy(ident16[:], ident[:])
            dve.tensor_copy(ident_bf[:], ident[:])
            link(dve.memset(count[:], 0.0))

            def nothing(j=None):
                pass

            def moments(source, ready=nothing):
                for j in range(TB):
                    ready(j)
                    last = dve.bn_stats(stats[:, j, :], source(j))
                link(last, apart)
                for j in range(TB):
                    last = dve.bn_aggr(mv[:, j, :], stats[:, j, :])
                link(last)

            def set_up():
                dve.wait_ge(setup_loaded, 16 * 5)
                link(dve.tensor_scalar(norm_scaled[:], norm[:], W_SCALE, None, ALU.mult))
                link(dve.tensor_reduce(wo_mean[:], wo_raw, AX_X, ALU.add))
                link(dve.tensor_scalar(wo_mean[:], wo_mean[:], -1.0 / D, None, ALU.mult))
                for c in range(C):
                    link(dve.tensor_scalar(wos[:, c, :], wo_raw[:, c, :], wo_mean[:, c:c + 1], None, ALU.add))
                dve.wait_ge(setup_turned, 2)
                for h in range(C):
                    last = dve.tensor_scalar(gateT[:, h, :], bank[7][:, h * E:(h + 1) * E], norm[:, h:h + 1],
                                             1.0 / U_SCALE, ALU.mult, ALU.mult)
                last.then_inc(setup_done, 1)

            def split_biases():
                dve.wait_ge(bias_loaded, 16 * 3)
                dve.wait_ge(setup_done, 1)
                b1_out = bias_t[:, 0:O].rearrange("p (c i) -> p c i", c=2)
                b1_in = bias_f[:, 0:O].rearrange("p (i c) -> p c i", c=2)
                link(dve.tensor_scalar(b1_out, b1_in, H_SCALE, None, ALU.mult))
                link(dve.tensor_copy(bias_rows[:, :], bias_t))
                for n, q in enumerate((32, 64, 64)):
                    rest, part_rows = bias_t[q:q + 32, :], bias_rows[q:q + 32, :]
                    link(dve.tensor_tensor(rest, rest, part_rows, ALU.subtract))
                    dve.tensor_copy(part_rows, rest).then_inc(bias_ready, 1)
                    dve.wait_ge(bias_ready, n + 1)

            def ask_power(value, scale, which=0):
                dve.tensor_scalar(var_eps[:, which, :], value, scale, EPS, ALU.mult, ALU.add).then_inc(var_ready, 1)

            def power(value, scale, n, meanwhile=nothing):
                ask_power(value, scale)
                meanwhile()
                dve.wait_ge(rstd_ready, n)

            def norm_stats(b, side, loaded=nothing):
                moments(lambda j: tile_x(b % B, j), loaded)
                dve.tensor_copy(x_mean[:, side, :], mv[:, :, 0])
                dve.tensor_scalar(x_mean_neg[:, bass.ds(b * TB, TB)], mv[:, :, 0], -1.0, None, ALU.mult)
                ask_power(mv[:, :, 1], 1.0, 1)

            def norm_of(b, side, n):
                dve.wait_ge(rstd_ready, n)
                for j in range(TB):
                    dve.tensor_scalar(turn_of(side, j), tile_x(b, j), mv[:, j, 0:1], rstd_next[:, j:j + 1],
                                      ALU.subtract, ALU.mult).then_inc(xn_ready, 1)

            def softmax_of(b, meanwhile=nothing):
                dve.wait_ge(scores_done, b + 1)
                link(dve.tensor_reduce(row_max[:], bank[4][:, :].rearrange("p (c d) -> p c d", c=C), AX_X, ALU.max))
                dve.tensor_scalar(row_neg[:], row_max[:], -SCORE_SCALE, None, ALU.mult).then_inc(max_ready, 1)
                meanwhile()
                dve.wait_ge(exp_done, b + 1)
                link(dve.reciprocal(row_inv[:], row_sum[:]))
                for c in range(C):
                    last = dve.tensor_scalar(probs[:, c, :], probs[:, c, :], row_inv[:, c:c + 1], None, ALU.mult)
                last.then_inc(probs_ready, 1)

            def attention_added(b, n, meanwhile):
                dve.wait_ge(squared, 2 * TB * b + TB)
                power(squares[:, 0, :], 1.0 / D, n, meanwhile=meanwhile)
                for j in range(TB):
                    dve.scalar_tensor_tensor(out=tile_x(b, j), in0=halves(j // 2)[j % 2], scalar=rstd[:, j:j + 1],
                                             in1=tile_x(b, j), op0=ALU.mult, op1=ALU.add).then_inc(x_added, 1)

            def u_of(b, side, n, next_batch, meanwhile):
                dve.wait_ge(squared, 2 * TB * (b + 1))
                dve.tensor_scalar(var_eps[:, 0, :], squares[:, 1, :], (1.0 + EPS) / D / U_SCALE ** 2,
                                  (EPS / U_SCALE) ** 2, ALU.mult, ALU.add).then_inc(var_ready, 1)
                dve.tensor_scalar(ffn_rstd[:, bass.ds(b * TB, TB)], squares[:, 1, :], 1.0 / D, EPS, ALU.mult, ALU.add)
                meanwhile()
                dve.wait_ge(rstd_ready, n)
                if next_batch:
                    dve.wait_ge(xn_turned, TB // 2 * (b + 2))
                for j in range(TB):
                    dve.tensor_scalar(turn_of(side, j), tile_x(b, j), x_mean[:, 1 - side, j:j + 1], rstd[:, j:j + 1],
                                      ALU.subtract, ALU.mult).then_inc(u_ready, 1)

            def chosen_experts(b):
                return top_e[:, bass.ds(b * (TB * TOP), TB * TOP)]

            def mark_experts(b):
                link(dve.tensor_tensor(onehot[:], chosen_experts(b).unsqueeze(2).to_broadcast([P, TB * TOP, E]),
                                       expert_no[:, :].unsqueeze(1).to_broadcast([P, TB * TOP, E]), ALU.is_equal))

            def choose(b, meanwhile):
                dve.wait_ge(logits_done, TB // 2 * (b + 1))
                link(dve.tensor_tensor(logits[:], bank[0][:, 0:TB * E].rearrange("p (j e) -> p j e", e=E),
                                       gate_b_all[:, :].unsqueeze(1).to_broadcast([P, TB, E]), ALU.add), apart)
                for j in range(TB):
                    last = dve.max(top_v[:, j, :], logits[:, j, :])
                link(last)
                dve.tensor_tensor(gate_e[:], top_v[:, :, 0:TOP], top_v[:, :, 0:1].to_broadcast([P, TB, TOP]),
                                  ALU.subtract).then_inc(gate_in_ready, 1)
                for j in range(TB):
                    last = dve.max_index(top_i[:, j, :], top_v[:, j, :], logits[:, j, :])
                link(last)
                link(dve.tensor_copy(chosen_experts(b).rearrange("p (j k) -> p j k", k=TOP), top_i[:, :, 0:TOP]))
                mark_experts(b)
                by_expert = onehot[:].rearrange("p (j k) e -> p j e k", k=TOP)
                with nc.allow_low_precision("sums of at most four ones"):
                    dve.tensor_reduce(chosen[:], by_expert, AX_X, ALU.add).then_inc(chosen_ready, 1)
                link(dve.tensor_reduce(batch_count[:], onehot[:].rearrange("p t e -> p e t"), AX_X, ALU.add))
                meanwhile()

            def gates_of(b):
                dve.wait_ge(gate_exp_done, b + 1)
                link(dve.tensor_reduce(gate_sum[:], gate_e[:], AX_X, ALU.add))
                link(dve.reciprocal(gate_inv[:], gate_sum[:]))
                own = gates[:, bass.ds(b * (TB * TOP), TB * TOP)].rearrange("p (j k) -> p j k", k=TOP)
                link(dve.scalar_tensor_tensor(out=own, in0=gate_e[:], scalar=1.0 / Y_SCALE,
                                              in1=gate_inv[:, :].unsqueeze(2).to_broadcast([P, TB, TOP]),
                                              op0=ALU.mult, op1=ALU.mult))

            def places_of(b, side):
                dve.wait_ge(rank_done, b + 1)
                ranks = bank[1][:, 0:TB * E].rearrange("p (j e) -> p j e", e=E)
                for j in range(TB):
                    one = onehot[:, j * TOP:(j + 1) * TOP, :]
                    last = dve.tensor_tensor(one, one, ranks[:, j:j + 1, :].to_broadcast([P, TOP, E]), ALU.mult)
                link(last)
                dve.tensor_tensor(count[:], count[:], batch_count[:], ALU.add).then_inc(counted, 1)
                link(dve.tensor_reduce(rank[:], onehot[:], AX_X, ALU.add))
                link(dve.scalar_tensor_tensor(out=row_f[:], in0=chosen_experts(b), scalar=float(REGION), in1=rank[:],
                                              op0=ALU.mult, op1=ALU.add))
                link(dve.tensor_copy(row_i[:, side, :], row_f[:]))

            def stage_rows(b, side, j):
                dve.wait_ge(hi_staged, TB * b + j + 1)
                to = stage[:, j % 2]
                own = to[:, 0, 0:D].bitcast(F16)
                dve.tensor_tensor(own[:, D:2 * D], turn_of(side, j), own[:, 0:D], ALU.subtract)
                dve.tensor_copy(to[:, :, TOKEN].bitcast(I32), token[:, bass.ds(b * TB + j, 1)].to_broadcast([P, TOP]))
                link(dve.tensor_copy(to[:, :, GATE], gates[:, bass.ds(b * (TB * TOP) + j * TOP, TOP)]))
                dve.tensor_copy(to[:, 1:TOP, 0:D].bitcast(F16),
                                own.unsqueeze(1).to_broadcast([P, TOP - 1, 2 * D])).then_inc(staged, 1)

            def low_weights(i, n):
                part_no, at = n % 3, i * (4 * WE) + n // 3 * WE
                dve.wait_ge(w_high, FILLS * i + n + 1)
                if part_no < C:
                    high, low = (W[:, bass.ds(at + k * W1PART + part_no * O, O)] for k in range(2))
                    scale = norm_scaled[:, part_no:part_no + 1]
                else:
                    high, low = (W[:, bass.ds(at + 2 * W1PART + k * W2PART, W2PART)] for k in range(2))
                    scale = W_SCALE
                dve.scalar_tensor_tensor(out=low, in0=bank[6 + n % 2][:, :], scalar=scale, in1=high,
                                         op0=ALU.mult, op1=ALU.subtract).then_inc(w_low, 1)

            def front(i, side, next_batch=True, last_batch=True):
                def fill(rows_of=None, weights_of=()):
                    if last_batch and rows_of is not None:
                        stage_rows(i - 1, 1 - side, rows_of)
                    for n in weights_of:
                        low_weights(i, n)

                if next_batch:
                    norm_of(i + 1, side, 3 * i + 2)
                fill(2, (0, 1))
                attention_added(i, 3 * i + 3, lambda: fill(3, (2, 3)))
                u_of(i, side, 3 * i + 4, next_batch, lambda: fill(4))
                fill(5)
                if next_batch:
                    softmax_of(i + 1, meanwhile=lambda: norm_stats(i + 2, 1 - side))
                fill(6)
                choose(i, lambda: fill(7, (4, 5)))
                gates_of(i)
                places_of(i, side)
                fill(None, (6,))
                stage_rows(i, side, 0)
                fill(None, (7, 8))
                stage_rows(i, side, 1)
                fill(None, range(9, FILLS))

            def loaded(b):
                def wait_for(j):
                    if j % (TB // 2) == 0:
                        dve.wait_ge(x_loaded[j // (TB // 2)], 16 * (b + 1))
                return wait_for

            norm_stats(0, 1, loaded(0))
            set_up()
            norm_of(0, 1, 1)
            norm_stats(1, 0, loaded(1))
            split_biases()
            for n in range(2):
                dve.wait_ge(x_loaded[n], 16 * B)
            softmax_of(0)
            before = steps.n
            front(0, 0, last_batch=False)
            per_batch = steps.n - before + TB - 2
            start = steps.passed()
            with dve.Fori(0, (B - 2) // 2) as k:
                steps.base, steps.n = k * (2 * per_batch) + start, 0
                front(2 * k + 1, 1)
                front(2 * k + 2, 0)
                assert steps.n == 2 * per_batch
            steps.base, steps.n = start + (B - 2) * per_batch, 0
            front(B - 1, (B - 1) % 2, next_batch=False)

            def paddings():
                dve.wait_ge(counts_done, 1)
                link(dve.tensor_tensor(pad_f[:, 0:E], counts[0:1, :], pad_base[:, 0:E], ALU.add))
                link(dve.tensor_copy(pad_f[:, E:E + 1], pad_base[:, E:E + 1]))
                dve.tensor_copy(pad_row[:], pad_f[:]).then_inc(pad_ready, 1)

            def tile_sums():
                link(dve.tensor_scalar(tile_f[:], counts, float(P - 1), None, ALU.add))
                link(dve.tensor_copy(tile_i[:], tile_f[:]))
                link(dve.tensor_scalar(tile_i[:], tile_i[:], P.bit_length() - 1, None, ALU.logical_shift_right))
                link(dve.tensor_copy(cum[:, 0, :], tile_i[:]))
                at, shift = 0, 1
                while shift < E:
                    dve.tensor_copy(cum[:, 1 - at, 0:shift], cum[:, at, 0:shift])
                    link(dve.tensor_tensor(cum[:, 1 - at, shift:E], cum[:, at, shift:E], cum[:, at, 0:E - shift],
                                           ALU.add))
                    at, shift = 1 - at, 2 * shift
                return cum[0:1, at, :].unsqueeze(1).to_broadcast([1, STEPS, E])

            def experts_ahead(tiles_up_to):
                link(dve.tensor_tensor(table, tiles_up_to, no.unsqueeze(2).to_broadcast([1, STEPS, E]), ALU.is_le))

            def step_experts():
                link(dve.tensor_reduce(step_e, table, AX_X, ALU.add))

            def tiles_ahead(tiles_up_to):
                link(dve.tensor_tensor(table, table, tiles_up_to, ALU.mult))

            def step_tiles():
                link(dve.tensor_reduce(step_t, table, AX_X, ALU.max))
                link(dve.tensor_tensor(step_t, no, step_t, ALU.subtract))

            def step_addresses():
                link(dve.tensor_scalar(step_x, step_e, float(REGION), None, ALU.mult))
                link(dve.scalar_tensor_tensor(out=step_x, in0=step_t, scalar=float(P), in1=step_x, op0=ALU.mult,
                                              op1=ALU.add))
                link(dve.tensor_scalar(step_x, step_x, float(ROW_MAX), None, ALU.min))
                dve.tensor_copy(step_row[:], step_x)
                link(dve.tensor_scalar(step_e, step_e, float(E - 1), None, ALU.min))
                link(dve.tensor_scalar(step_t, step_e, float(WE), None, ALU.mult))
                dve.tensor_copy(step_at[:], step_t).then_inc(tables_ready, 1)

            counts = bank[5][:, 0:E]
            no = step_no[:]
            paddings()
            last_side = (B - 1) % 2
            stage_rows(B - 1, last_side, 2)
            tiles_up_to = tile_sums()
            stage_rows(B - 1, last_side, 3)
            experts_ahead(tiles_up_to)
            stage_rows(B - 1, last_side, 4)
            step_experts()
            stage_rows(B - 1, last_side, 5)
            tiles_ahead(tiles_up_to)
            stage_rows(B - 1, last_side, 6)
            step_tiles()
            stage_rows(B - 1, last_side, 7)
            step_addresses()

            for b in range(B):
                mark_experts(b)
                of = gates[:, b * TB * TOP:(b + 1) * TB * TOP]
                link(dve.tensor_tensor(onehot[:], onehot[:], of.unsqueeze(2).to_broadcast([P, TB * TOP, E]), ALU.mult))
                by_expert = onehot[:].rearrange("p (j k) e -> p j e k", k=TOP)
                dve.tensor_reduce(gate_cols[:, b * TB:(b + 1) * TB], by_expert, AX_X,
                                  ALU.add).then_inc(gate_cols_ready, 1)
                dve.wait_ge(gate_cols_ready, b + 1)

            dve.wait_ge(b2_loaded, 16 * (P // E))
            link(dve.tensor_scalar(b2_f, b2_f, Y_SCALE, None, ALU.mult))
            link(dve.tensor_copy(b2_parts, b2_f))
            for n, q in enumerate((P // 4, P // 2, P // 2)):
                rest, part_rows = b2_f[q:q + P // 4, :], b2_parts[q:q + P // 4, :]
                link(dve.tensor_tensor(rest, rest, part_rows, ALU.subtract))
                if n < 2:
                    link(dve.tensor_copy(part_rows, rest))
                else:
                    dve.tensor_copy(part_rows, rest).then_inc(b2_ready, 1)

            def low(s, r):
                dve.wait_ge(high_ready, s + 1)
                dve.tensor_tensor(act_hl[:, r, D:2 * D], act_t[:, r, :], act_hl[:, r, 0:D],
                                  ALU.subtract).then_inc(low_ready, 1)

            def clip(s, r):
                h = bank[2 + r]
                dve.wait_ge(h_done, s + 1)
                dve.tensor_scalar(a_t[:, r, :], h[:, 0:D], 1.0 / H_SCALE, LIMIT, ALU.mult,
                                  ALU.min).then_inc(a_ready, 1)
                dve.tensor_scalar(b_t[:, r, :], h[:, D:2 * D], LIMIT * H_SCALE, -LIMIT * H_SCALE, ALU.min,
                                  ALU.max).then_inc(h_used, 1)

            def act_out(s, r):
                dve.wait_ge(act_turned, s + 1)
                wait(dve, y_done, s - 1)
                dve.tensor_copy(actT[:, r, :], bank[4 + r][:, :].bitcast(F16)[:, 0:4 * P]).then_inc(act_copied, 1)

            def activate(s, r):
                dve.wait_ge(h_used, s + 1)
                dve.scalar_tensor_tensor(out=m_t[:, r, :], in0=b_t[:, r, :], scalar=H_SCALE, in1=a_t[:, r, :],
                                         op0=ALU.add, op1=ALU.mult).then_inc(m_ready, 1)
                dve.wait_ge(sig_ready, s + 1)
                dve.wait_ge(m_ready, s + 1)
                dve.scalar_tensor_tensor(out=act_t[:, r, :], in0=m_t[:, r, :], scalar=A_SCALE / H_SCALE,
                                         in1=sig_t[:, r, :], op0=ALU.mult, op1=ALU.mult).then_inc(act_ready, 1)

            def step(m, c):
                s = m * RING + c
                if live(s - TURN):
                    low(s - TURN, (c - TURN) % 2)
                if live(s - FIRST):
                    clip(s - FIRST, (c - FIRST) % 2)
                if live(s - TURN):
                    act_out(s - TURN, (c - TURN) % 2)
                if live(s - FIRST):
                    activate(s - FIRST, (c - FIRST) % 2)

            for c in range(RING):
                step(0, c)
            with dve.Fori(1, ROUNDS) as m:
                for c in range(RING):
                    step(m, c)
            for c in range(TURN):
                step(ROUNDS, c)

            dve.wait_ge(gate_parts_zeroed, 1)
            for b in range(B):
                at = slice(b * TB, (b + 1) * TB)
                rest, quarters = gate_cols[:, at], gate_quarters[:, at]
                for i in range(2):
                    link(dve.tensor_copy(quarters[:, :, 0, i, :], rest))
                    for q in range(1, 3):
                        dve.tensor_copy(quarters[:, :, q, i, :], rest)
                    link(dve.tensor_tensor(rest, rest, quarters[:, :, 0, i, :], ALU.subtract))
                dve.tensor_copy(quarters[:, :, 3, 0, :], rest).then_inc(gate_parts_ready, 1)

            def finish(b, n):
                wait(dve, out_stored[n], 16 * b)
                for j in HALF[n]:
                    dve.wait_ge(scaled, TB * b + j + 1)
                    dve.tensor_tensor(fin[:, j, :], scaled_t[:, j, :], tile_x(b, j), ALU.add).then_inc(finished, 1)

            def end(b, n, finish_last=True):
                for j in HALF[n]:
                    dve.wait_ge(ffn_summed, TB * b + j + 1)
                    apart(dve)
                    last = dve.bn_stats(stats[:, j, :], bank[j][:, 0:D])
                link(last, apart)
                for j in HALF[n]:
                    last = dve.bn_aggr(mv[:, j, :], stats[:, j, :])
                link(last)
                of = slice(HALF[n][0], HALF[n][-1] + 1)
                dve.tensor_scalar(var_eps[:, 0, of], mv[:, of, 1], EPS, None, ALU.add).then_inc(var_ready, 1)
                if finish_last:
                    finish(b - 1 + n, 1 - n)
                dve.wait_ge(rstd_ready, POWERS + 2 * b + n + 1)
                dve.scalar_tensor_tensor(out=end_bias[:, of], in0=mv[:, of, 0], scalar=-1.0, in1=rstd[:, of],
                                         op0=ALU.mult, op1=ALU.mult).then_inc(ffn_scale_ready, 1)

            for c in range(RING):
                dve.wait_ge(result_sent[c], 16 * ROUNDS)
            start = steps.passed()
            end(0, 0, finish_last=False)
            end(0, 1)
            per_batch = steps.n
            for n in range(2):
                end(1, n)
            with dve.Fori(2, B) as b:
                steps.base, steps.n = b * per_batch + start, 0
                for n in range(2):
                    end(b, n)
            finish(B - 1, 1)


_INS = ["L0_attn_x", "L0_attn_Wq", "L0_attn_Wk", "L0_attn_Wv", "L0_attn_Wo", "L0_ffn_norm_w", "L0_ffn_gate_w",
        "L0_ffn_gate_b", "L0_ffn_w1", "L0_ffn_b1", "L0_ffn_w2", "L0_ffn_b2"]


def kernel(**inputs):
    import numpy as np
    import concourse.bacc as bacc
    from concourse.bass_utils import run_bass_kernel_spmd

    nc = bacc.Bacc("TRN2", target_bir_lowering=False, num_devices=1)
    arrays, args = {}, []
    for name in _INS:
        a = np.ascontiguousarray(inputs[name])
        arrays[f"in_{name}"] = a
        args.append(nc.dram_tensor(f"in_{name}", a.shape, mybir.dt.from_np(a.dtype), kind="ExternalInput").ap())
    out = nc.dram_tensor("out", arrays["in_L0_attn_x"].shape, F32, kind="ExternalOutput").ap()
    moe_block(nc, *args, out)
    r = run_bass_kernel_spmd(nc, [arrays], core_ids=[0])
    return r.results[0]["out"]
```
